# Optimizing a Trainium2 kernel written in Bass

```python
import numpy as np
import jax
import jax.numpy as jnp

def _softmax(x, axis=-1):
    return jax.nn.softmax(x, axis=axis)
def _gelu(x):
    return jax.nn.gelu(x, approximate=True)
def _silu(x):
    return jax.nn.silu(x)
def _sigmoid(x):
    return jax.nn.sigmoid(x)
def _layernorm(x, axis=-1, eps=1e-5):
    m = jnp.mean(x, axis=axis, keepdims=True)
    v = jnp.var(x, axis=axis, keepdims=True)
    return (x - m) / jnp.sqrt(v + eps)
def _scatter_add(tgt, idx, src, axis=0):
    return tgt.at[idx].add(src)
def _segment_sum(src, seg, n):
    return jax.ops.segment_sum(src, seg, n)

kernel_name = 'mk_conv_seq_d1_conv_nchw512_aa349c'

def setup_inputs(seed: int = 0):
    np.random.seed(seed)
    _w = jnp.asarray
    def _rec_inputs():
        import jax
        import jax.numpy as jnp
        _gk = jax.random.key(seed)
        x = -0.000125 + 0.9999 * jax.random.normal(jax.random.fold_in(_gk, 1), (4, 512, 128, 128), jnp.float32)
        return x
    x = _rec_inputs()
    def _L0_conv_setup():
        import jax, jax.numpy as jnp
        import numpy as np
        DIM = 512
        NB = 8
        BS = DIM // NB
        MODES = (64, 33)
        LAM = 0.01
        B, H, W = (4, 128, 128)

        def _complex_linear(zr, zi, wr, wi, br, bi):
            yr = jnp.einsum('bhwni,nij->bhwnj', zr, wr) - jnp.einsum('bhwni,nij->bhwnj', zi, wi) + br
            yi = jnp.einsum('bhwni,nij->bhwnj', zr, wi) + jnp.einsum('bhwni,nij->bhwnj', zi, wr) + bi
            return (yr, yi)

        def _softshrink(y, lam):
            return jnp.sign(y) * jnp.maximum(jnp.abs(y) - lam, 0.0)
        key = jax.random.key(seed)
        ks = jax.random.split(key, 10)
        f32 = jnp.float32
        return {'x': jax.random.normal(ks[0], (B, DIM, H, W), dtype=f32), 'w1_real': jax.random.normal(ks[1], (NB, BS, BS), dtype=f32) * 0.02, 'w1_imag': jax.random.normal(ks[2], (NB, BS, BS), dtype=f32) * 0.02, 'b1_real': jax.random.normal(ks[3], (NB, BS), dtype=f32) * 0.02, 'b1_imag': jax.random.normal(ks[4], (NB, BS), dtype=f32) * 0.02, 'w2_real': jax.random.normal(ks[5], (NB, BS, BS), dtype=f32) * 0.02, 'w2_imag': jax.random.normal(ks[6], (NB, BS, BS), dtype=f32) * 0.02, 'b2_real': jax.random.normal(ks[7], (NB, BS), dtype=f32) * 0.02, 'b2_imag': jax.random.normal(ks[8], (NB, BS), dtype=f32) * 0.02, 'fuse_w': jax.random.normal(ks[9], (DIM, DIM), dtype=f32) * 0.02}
    _L0_conv_all = _L0_conv_setup()
    _L0_conv_in = {k: v for k, v in _L0_conv_all.items() if k in ('w1_real', 'w1_imag', 'b1_real', 'b1_imag', 'w2_real', 'w2_imag', 'b2_real', 'b2_imag', 'fuse_w', )}
    del _L0_conv_all

    return {
        "x": x,
        "L0_conv_w1_real": _L0_conv_in["w1_real"],
        "L0_conv_w1_imag": _L0_conv_in["w1_imag"],
        "L0_conv_b1_real": _L0_conv_in["b1_real"],
        "L0_conv_b1_imag": _L0_conv_in["b1_imag"],
        "L0_conv_w2_real": _L0_conv_in["w2_real"],
        "L0_conv_w2_imag": _L0_conv_in["w2_imag"],
        "L0_conv_b2_real": _L0_conv_in["b2_real"],
        "L0_conv_b2_imag": _L0_conv_in["b2_imag"],
        "L0_conv_fuse_w": _L0_conv_in["fuse_w"],
    }

def reference(x, L0_conv_w1_real, L0_conv_w1_imag, L0_conv_b1_real, L0_conv_b1_imag, L0_conv_w2_real, L0_conv_w2_imag, L0_conv_b2_real, L0_conv_b2_imag, L0_conv_fuse_w):
    import jax
    import jax.numpy as jnp
    def _L0_conv_ref(x, w1_real, w1_imag, b1_real, b1_imag, w2_real, w2_imag, b2_real, b2_imag, fuse_w):
        import jax, jax.numpy as jnp
        import numpy as np
        DIM = 512
        NB = 8
        BS = DIM // NB
        MODES = (64, 33)
        LAM = 0.01
        B, H, W = (4, 128, 128)

        def _complex_linear(zr, zi, wr, wi, br, bi):
            yr = jnp.einsum('bhwni,nij->bhwnj', zr, wr) - jnp.einsum('bhwni,nij->bhwnj', zi, wi) + br
            yi = jnp.einsum('bhwni,nij->bhwnj', zr, wi) + jnp.einsum('bhwni,nij->bhwnj', zi, wr) + bi
            return (yr, yi)

        def _softshrink(y, lam):
            return jnp.sign(y) * jnp.maximum(jnp.abs(y) - lam, 0.0)
        b, c, h, w = x.shape
        Z = jnp.fft.rfft2(x, axes=(-2, -1), norm='ortho')
        Hf, Wf = (Z.shape[-2], Z.shape[-1])
        Zr = jnp.transpose(Z.real.reshape(b, NB, BS, Hf, Wf), (0, 3, 4, 1, 2))
        Zi = jnp.transpose(Z.imag.reshape(b, NB, BS, Hf, Wf), (0, 3, 4, 1, 2))
        hr, hi = _complex_linear(Zr, Zi, w1_real, w1_imag, b1_real, b1_imag)
        hr = jax.nn.gelu(hr, approximate=False)
        hi = jax.nn.gelu(hi, approximate=False)
        yr, yi = _complex_linear(hr, hi, w2_real, w2_imag, b2_real, b2_imag)
        yr = _softshrink(yr, LAM)
        yi = _softshrink(yi, LAM)
        m1, m2 = (min(MODES[0], Hf), min(MODES[1], Wf))
        mask = jnp.zeros((Hf, Wf), dtype=bool).at[:m1, :m2].set(True)[None, :, :, None, None]
        Zr_out = jnp.where(mask, yr, Zr)
        Zi_out = jnp.where(mask, yi, Zi)
        Zr_out = jnp.transpose(Zr_out, (0, 3, 4, 1, 2)).reshape(b, c, Hf, Wf)
        Zi_out = jnp.transpose(Zi_out, (0, 3, 4, 1, 2)).reshape(b, c, Hf, Wf)
        y = jnp.fft.irfft2(Zr_out + 1j * Zi_out, s=(h, w), axes=(-2, -1), norm='ortho')
        y = jnp.einsum('oc,bchw->bohw', fuse_w, y)
        return x + y

    def _gn(v, G=32, eps=1e-5):
        B_, C_, H_, W_ = v.shape
        g = v.reshape(B_, G, C_ // G, H_, W_)
        m = jnp.mean(g, axis=(2, 3, 4), keepdims=True)
        s = jnp.var(g, axis=(2, 3, 4), keepdims=True)
        return ((g - m) / jnp.sqrt(s + eps)).reshape(v.shape)

    def _ln_c(v, eps=1e-6):
        m = jnp.mean(v, axis=1, keepdims=True)
        s = jnp.var(v, axis=1, keepdims=True)
        return (v - m) / jnp.sqrt(s + eps)

    def _ln_t(v, eps=1e-5):
        m = jnp.mean(v, axis=-1, keepdims=True)
        s = jnp.var(v, axis=-1, keepdims=True)
        return (v - m) / jnp.sqrt(s + eps)

    def _to_tokens(v):
        B_, C_, H_, W_ = v.shape
        return v.reshape(B_, C_, H_ * W_).transpose(0, 2, 1)
    def _from_tokens(t, like):
        B_, C_, H_, W_ = like.shape
        return t.transpose(0, 2, 1).reshape(B_, C_, H_, W_)

    x = _L0_conv_ref(x, L0_conv_w1_real, L0_conv_w1_imag, L0_conv_b1_real, L0_conv_b1_imag, L0_conv_w2_real, L0_conv_w2_imag, L0_conv_b2_real, L0_conv_b2_imag, L0_conv_fuse_w)
    return x


_drawn_inputs = setup_inputs


def setup_inputs(seed=0):
    import zlib

    import numpy as np

    out = dict(_drawn_inputs(seed))
    spreads = {}
    factors = {'L0_conv_w1_real': 8.0,
     'L0_conv_w1_imag': 8.0,
     'L0_conv_b1_real': 8.0,
     'L0_conv_b1_imag': 8.0,
     'L0_conv_w2_real': 8.0,
     'L0_conv_w2_imag': 8.0,
     'L0_conv_b2_real': 8.0,
     'L0_conv_b2_imag': 8.0}
    for name, (base, spread) in spreads.items():
        noise = np.random.default_rng([zlib.crc32(name.encode()), seed]).standard_normal(out[name].shape)
        drawn = base * np.exp(spread * noise) if base else spread * noise
        out[name] = jnp.asarray(drawn.astype(out[name].dtype))
    for name, factor in factors.items():
        out[name] = (out[name] * factor).astype(out[name].dtype)
    return out
```

```python
import concourse.bass as bass
from concourse import mybir
from contextlib import ExitStack

B, C, H, W = 4, 512, 128, 128
NB, BS = 8, 64
KH, KW = 64, 33
LAM = 0.01
P = 128
CB = C // P
R2 = 2 * KW

XC = 8
XB = 4
S1_JOBS = P // 8
S2_JOBS = KH // 8
HC = 8
L_JOBS = KH // HC
T_JOBS = (KW + 7) // 8
I1_KW = 3
I1_JOBS = KW // I1_KW
ECH = 3

TH = 4
TP = TH * W
TILES = H // TH
UN = 4


def job_order():
    jobs = [("s1", j) for j in range(S1_JOBS)] + [("s2", j) for j in range(S2_JOBS)]
    jobs.append(("l1", 0))
    for j in range(1, L_JOBS):
        jobs += [("l1", j), ("l2", j - 1)]
    jobs.append(("l2", L_JOBS - 1))
    jobs += [("t", j) for j in range(T_JOBS)] + [("i1", j) for j in range(I1_JOBS)]
    return jobs


JOBS = job_order()
NJ = len(JOBS)
AT = {job: k for k, job in enumerate(JOBS)}
assert NJ % 4 == 0


def spectral_mix(nc, x, w1r, w1i, w2r, w2i, bias, fuse_t, const, out, spill):
    fp32 = mybir.dt.float32
    fp32r = mybir.dt.float32r
    ALU = mybir.AluOpType
    ACT = mybir.ActivationFunctionType

    x_rows = x.rearrange("b (k c) h w -> (b k) h c w", c=P)
    x_pix = x.rearrange("b (k c) h w -> b c k (h w)", c=P)
    out_pix = out.rearrange("b (k c) h w -> b c k (h w)", c=P)
    spill_r = spill.rearrange("b h m c -> b m h c")

    with ExitStack() as ctx:
        def sb(name, shape, dt=fp32):
            return ctx.enter_context(nc.sbuf_tensor(name, shape, dt))

        def sem(name):
            return ctx.enter_context(nc.semaphore(name))

        cst = sb("cst", [P, 772])
        f_h, f_wr, f_wi = cst[:, 0:128], cst[:, 128:194], cst[:, 194:260]
        g_hr, g_hi, g_w, ident = cst[:, 260:388], cst[:, 388:516], cst[0:R2, 516:644], cst[:, 644:772]
        fuse_hi = sb("fuse_hi", [P, CB, C], fp32r)
        fuse_lo = sb("fuse_lo", [P, CB, C], fp32r)

        mlp_w = sb("mlp_w", [P, 6, P])
        mlp_b = sb("mlp_b", [P, 4])
        xin = sb("xin", [P, XB, XC, W])
        zero = sb("zero", [P, P])
        spill_mark = sb("spill_mark", [P, 1])
        big = sb("big", [P, P * P])
        A = big[:, :].rearrange("p (c k) -> p c k", c=P)
        xt = big[:, 0:4 * CB * TP].rearrange("p (n k q) -> p n k q", n=4, k=CB)
        et = big[0:R2, 4 * CB * TP:6 * CB * TP].rearrange("p (n h c) -> p n h c", n=2, h=TH)
        ot = big[:, 6 * CB * TP:8 * CB * TP].rearrange("p (n k q) -> p n k q", n=2, k=CB)
        modes = sb("modes", [P, 2, KH, KW])
        u = modes[:, :, :, :].rearrange("p r a b -> p (r a b)")[:, 0:2 * CB * TP].rearrange("p (n q) -> p n q", q=TP)
        modes_v = modes[:, :, :, :].rearrange("p r h m -> p r (h m)")
        modes_k = modes[:, :, :, :].rearrange("p r h m -> p (r h) m")
        fuse_raw = big[:, 0:CB * C].rearrange("p (k o) -> p k o", k=CB)
        hid = sb("hid", [P, 2, 2, HC * KW])
        yt = sb("yt", [P, 2, 2, HC * KW])
        clip = sb("clip", [P, 2, HC * KW])
        ymz = sb("ymz", [P, 2, 2, HC * KW])
        V = sb("V", [P, KW, P])
        E = sb("E", [P, ECH, 2, I1_KW * P])
        u_hi = sb("u_hi", [P, 2, CB, TP], fp32r)
        u_lo = sb("u_lo", [P, 2, CB, TP], fp32r)
        ps = ctx.enter_context(nc.psum_tensor("ps", [P, 8, 512], fp32))

        def bank(k, half):
            return ps[:, 2 * (k % 4) + half, :]

        cst_in, fuse_in = sem("cst_in"), sem("fuse_in")
        fuse_hi_ready, fuse_lo_ready = sem("fuse_hi_ready"), sem("fuse_lo_ready")
        zeroed = sem("zeroed")
        w_in, b_in, wneg_ready = sem("w_in"), sem("b_in"), sem("wneg_ready")
        xin_in = [sem(f"xin_in{n}") for n in range(XB)]
        job_done = sem("job_done")
        evac = {n: sem(n) for n in ("a_act", "a_dve", "z_act", "z_dve", "h_act", "y_act",
                                    "v_act", "v_dve", "e_act", "e_dve")}
        PER = {"a_act": S1_JOBS, "a_dve": S1_JOBS, "z_act": S2_JOBS, "z_dve": S2_JOBS, "h_act": L_JOBS,
               "y_act": L_JOBS, "v_act": T_JOBS, "v_dve": T_JOBS - 1, "e_act": I1_JOBS, "e_dve": I1_JOBS}
        clip_ready, ymz_ready, d_ready = sem("clip_ready"), sem("ymz_ready"), sem("d_ready")
        spilled = [sem(f"spilled{n}") for n in range(ECH)]
        image_spilled = sem("image_spilled")
        xt_in = [sem(f"xt_in{n}") for n in range(4)]
        et_in = [sem(f"et_in{n}") for n in range(2)]
        i2_done, mix_done = sem("i2_done"), sem("mix_done")
        u_ready, uhi_ready, ulo_ready, out_ready = sem("u_ready"), sem("uhi_ready"), sem("ulo_ready"), sem("out_ready")
        stored = [sem(f"stored{n}") for n in range(2)]

        block = ctx.enter_context(nc.Block())

        def chunks_of(n):
            return len(range(n, I1_JOBS, ECH))

        def tile_bodies(eng, b, body):
            body(0, True, False)
            with eng.Fori(1, TILES // UN - 1) as q:
                body(q, False, False)
            body(TILES // UN - 1, False, True)

        @block.sync
        def _(sp):
            sp.dma_start(cst[:, :], const).then_inc(cst_in, 16)
            sp.dma_start(fuse_raw, fuse_t.rearrange("(k c) o -> c k o", c=P)).then_inc(fuse_in, 16)
            def load_chunk(g, j):
                sp.dma_start(xin[:, j % XB, :, :], x_rows[g, :, j * XC:(j + 1) * XC, :]).then_inc(xin_in[j % XB], 16)

            def load_rows(g, last):
                for j in range(XB, S1_JOBS if last else S1_JOBS + XB):
                    sp.wait_ge(job_done, g * NJ + (j - XB + 1))
                    load_chunk(g + j // S1_JOBS, j % S1_JOBS)

            with sp.Fori(0, B) as b:
                for j in range(XB):
                    load_chunk(b * CB, j)
                with sp.Fori(0, CB - 1) as cb:
                    load_rows(b * CB + cb, False)
                load_rows(b * CB + (CB - 1), True)
                sp.wait_ge(image_spilled, b + 1)

                def load_tiles(q, first, last):
                    for n in range(UN):
                        m = (b * TILES) + (q * UN + n)
                        if not first:
                            sp.wait_ge(out_ready, m * CB - (UN - 1) * CB)
                        sp.dma_start(xt[:, n, :, :], x_pix[b, :, :, bass.ds(q * (UN * TP) + n * TP, TP)]).then_inc(xt_in[n], 16)
                        if not first or n >= 2:
                            sp.wait_ge(i2_done, m * CB - CB)
                        sp.dma_start(et[:, n % 2, :, :], spill_r[b, :, bass.ds(q * (UN * TH) + n * TH, TH), :]).then_inc(et_in[n % 2], 16)

                tile_bodies(sp, b, load_tiles)

        @block.tensor
        def _(pe):
            mm = nc.tensor.matmul

            def taken(stage, j):
                n = j + 1
                return {"s1": {"a_act": n, "a_dve": n}, "s2": {"z_act": n, "z_dve": n}, "l1": {"h_act": n}, "l2": {"y_act": n},
                        "t": {"v_act": n, "v_dve": min(n, T_JOBS - 1)}, "i1": {"e_act": n, "e_dve": n}}[stage]

            def wait_for_job(g, k, inputs):
                before = taken(*JOBS[k - 4]) if k >= 4 else {}
                for name in {**before, **inputs}:
                    pe.wait_ge(evac[name], g * PER[name] + max(before.get(name, 0), inputs.get(name, 0)))

            pe.wait_ge(cst_in, 16)
            with pe.Fori(0, B) as b:
                with pe.Fori(0, CB) as cb:
                    g = b * CB + cb
                    for k, (stage, j) in enumerate(JOBS):
                        if stage == "s1":
                            wait_for_job(g, k, {})
                            pe.wait_ge(xin_in[j % XB], g * (S1_JOBS // XB * 16) + (j // XB + 1) * 16)
                            for i in range(8):
                                last = mm(bank(k, i // 4)[:, (i % 4) * P:(i % 4 + 1) * P],
                                          xin[:, j % XB, i, :], f_h, start=True, stop=True)
                        elif stage == "s2":
                            wait_for_job(g, k, taken("s1", S1_JOBS - 1))
                            for i in range(8):
                                kh = 8 * j + i
                                o = bank(k, i // 4)[:, (i % 4) * R2:(i % 4 + 1) * R2]
                                mm(o, A[:, :, kh], f_wr, start=True, stop=False)
                                last = mm(o, A[:, :, KH + kh], f_wi, start=False, stop=True)
                        elif stage == "l1":
                            if j == 0:
                                pe.wait_ge(wneg_ready, g * 2 + 2)
                            wait_for_job(g, k, taken("s2", j))
                            for ri, (wa, wb) in enumerate(((0, 2), (1, 0))):
                                o = bank(k, ri)[:, 0:HC * KW]
                                mm(o, mlp_w[:, wa, :], modes_v[:, 0, bass.ts(j, HC * KW)], start=True, stop=False)
                                last = mm(o, mlp_w[:, wb, :], modes_v[:, 1, bass.ts(j, HC * KW)], start=False, stop=True)
                        elif stage == "l2":
                            wait_for_job(g, k, taken("l1", j))
                            for ri, (wa, wb) in enumerate(((3, 5), (4, 3))):
                                o = bank(k, ri)[:, 0:HC * KW]
                                mm(o, mlp_w[:, wa, :], hid[:, j % 2, 0, :], start=True, stop=False)
                                last = mm(o, mlp_w[:, wb, :], hid[:, j % 2, 1, :], start=False, stop=True)
                        elif stage == "t":
                            wait_for_job(g, k, {})
                            if j == 0:
                                pe.wait_ge(d_ready, g * L_JOBS + L_JOBS)
                            for i in range(min(8, KW - 8 * j)):
                                last = nc.tensor.transpose(bank(k, i // 4)[:, (i % 4) * P:(i % 4 + 1) * P],
                                                           modes_k[:, :, 8 * j + i], ident)
                        else:
                            tj = (I1_KW * (j + 1) - 1) // 8
                            wait_for_job(g, k, taken("t", tj))
                            v = V[:, I1_KW * j:I1_KW * (j + 1), :]
                            mm(bank(k, 0)[:, 0:I1_KW * P], g_hr, v, start=True, stop=True)
                            last = mm(bank(k, 1)[:, 0:I1_KW * P], g_hi, v, start=True, stop=True)
                        last.then_inc(job_done, 1)
                    pe.wait_ge(evac["e_act"], g * I1_JOBS + I1_JOBS)
                    pe.wait_ge(evac["e_dve"], g * I1_JOBS + I1_JOBS)

                def inverse_w(m, n, first):
                    pe.wait_ge(et_in[n % 2], e_count(m, n))
                    for k in range(CB):
                        if not first:
                            pe.wait_ge(u_ready, m * CB - (CB - 1 - k))
                        for h in range(TH):
                            last = mm(ps[:, k, h * W:(h + 1) * W], et[:, n % 2, h, k * P:(k + 1) * P], g_w,
                                      start=True, stop=True)
                        last.then_inc(i2_done, 1)

                def e_count(m, n):
                    return m * 8 + (16 if n % 2 == 0 else 8)

                pe.wait_ge(fuse_hi_ready, 1)
                pe.wait_ge(fuse_lo_ready, 1)
                inverse_w(b * TILES, 0, True)

                def mix_tiles(q, first, last_body):
                    for n in range(UN):
                        m = (b * TILES) + (q * UN + n)
                        if not (last_body and n == UN - 1):
                            inverse_w(m + 1, n + 1, False)
                        for o in range(CB):
                            if not (first and n == 0):
                                pe.wait_ge(out_ready, m * CB - (CB - 1 - o))
                            for k in range(CB):
                                if o == 0:
                                    pe.wait_ge(uhi_ready, m * CB + (k + 1))
                                    pe.wait_ge(ulo_ready, m * CB + (k + 1))
                                w_hi, w_lo = fuse_hi[:, k, o * P:(o + 1) * P], fuse_lo[:, k, o * P:(o + 1) * P]
                                mm(ps[:, CB + o, :], w_hi, u_hi[:, n % 2, k, :], start=(k == 0), stop=False)
                                mm(ps[:, CB + o, :], w_hi, u_lo[:, n % 2, k, :], start=False, stop=False)
                                last = mm(ps[:, CB + o, :], w_lo, u_hi[:, n % 2, k, :], start=False, stop=(k == CB - 1))
                            last.then_inc(mix_done, 1)

                tile_bodies(pe, b, mix_tiles)
                pe.wait_ge(out_ready, (b + 1) * (TILES * CB))

        @block.scalar
        def _(act):
            act.wait_ge(fuse_in, 16)
            nc.scalar.activation(fuse_hi[:, :, :], fuse_raw, ACT.Copy).then_inc(fuse_hi_ready, 1)
            act.wait_ge(fuse_lo_ready, 1)
            with act.Fori(0, B) as b:
                with act.Fori(0, CB) as cb:
                    g = b * CB + cb
                    for k, (stage, j) in enumerate(JOBS):
                        act.wait_ge(job_done, g * NJ + (k + 1))
                        if stage == "s1":
                            nc.scalar.activation(A[:, 8 * j:8 * j + 4, :], bank(k, 0), ACT.Copy).then_inc(evac["a_act"], 1)
                        elif stage == "s2":
                            nc.scalar.activation(modes[:, :, 8 * j:8 * j + 4, :],
                                                 bank(k, 0)[:, 0:4 * R2].rearrange("p (h r m) -> p r h m", h=4, r=2),
                                                 ACT.Copy).then_inc(evac["z_act"], 1)
                        elif stage == "l1":
                            nc.scalar.activation(hid[:, j % 2, 0, :], bank(k, 0)[:, 0:HC * KW], ACT.Gelu, bias=mlp_b[:, 0:1])
                            nc.scalar.activation(hid[:, j % 2, 1, :], bank(k, 1)[:, 0:HC * KW], ACT.Gelu, bias=mlp_b[:, 1:2])\
                                .then_inc(evac["h_act"], 1)
                        elif stage == "l2":
                            if j >= 2:
                                act.wait_ge(clip_ready, g * L_JOBS + (j - 1))
                                act.wait_ge(ymz_ready, g * L_JOBS + (j - 1))
                            nc.scalar.activation(yt[:, j % 2, 0, :], bank(k, 0)[:, 0:HC * KW], ACT.Identity, bias=mlp_b[:, 2:3])
                            nc.scalar.activation(yt[:, j % 2, 1, :], bank(k, 1)[:, 0:HC * KW], ACT.Identity, bias=mlp_b[:, 3:4])\
                                .then_inc(evac["y_act"], 1)
                        elif stage == "t":
                            n = min(4, KW - 8 * j)
                            nc.scalar.activation(V[:, 8 * j:8 * j + n, :], bank(k, 0)[:, 0:n * P], ACT.Copy).then_inc(evac["v_act"], 1)
                        else:
                            if j >= ECH:
                                act.wait_ge(spilled[j % ECH], g * (chunks_of(j % ECH) * 32) + (j // ECH) * 32)
                            nc.scalar.activation(E[:, j % ECH, 0, :], bank(k, 0)[:, 0:I1_KW * P], ACT.Copy).then_inc(evac["e_act"], 1)

                    for n in range(ECH):
                        act.wait_ge(spilled[n], (g + 1) * (chunks_of(n) * 32))

                def upper_parts(m, n, reused):
                    for k in range(CB):
                        act.wait_ge(u_ready, m * CB + (k + 1))
                        if reused:
                            act.wait_ge(mix_done, m * CB - CB)
                        nc.scalar.activation(u_hi[:, n % 2, k, :], u[:, (n % 2) * CB + k, :], ACT.Copy).then_inc(uhi_ready, 1)

                upper_parts(b * TILES, 0, False)

                def tiles(q, first, last_body):
                    for n in range(UN):
                        m = (b * TILES) + (q * UN + n)
                        if not (last_body and n == UN - 1):
                            upper_parts(m + 1, n + 1, not (first and n == 0))

                tile_bodies(act, b, tiles)
                act.wait_ge(stored[0], (b + 1) * (TILES // 2 * 16))
                act.wait_ge(stored[1], (b + 1) * (TILES // 2 * 16))
                act.wait_ge(out_ready, (b + 1) * (TILES * CB))

        @block.vector
        def _(dve):
            dve.wait_ge(fuse_hi_ready, 1)
            nc.vector.tensor_tensor(fuse_lo[:, :, :], fuse_raw, fuse_hi[:, :, :].bitcast(fp32), ALU.subtract).then_inc(fuse_lo_ready, 1)
            dve.wait_ge(fuse_lo_ready, 1)
            with dve.Fori(0, B) as b:
                with dve.Fori(0, CB) as cb:
                    g = b * CB + cb
                    for k, (stage, j) in enumerate(JOBS):
                        if stage == "l1" or (stage, j) == ("t", T_JOBS - 1):
                            continue
                        if stage == "l2":
                            dve.wait_ge(evac["y_act"], g * L_JOBS + (j + 1))
                            if j:
                                dve.wait_ge(d_ready, g * L_JOBS + j)
                            nc.vector.tensor_scalar(clip[:, :, :], yt[:, j % 2, :, :], -LAM, LAM, ALU.max, ALU.min).then_inc(clip_ready, 1)
                            dve.wait_ge(clip_ready, g * L_JOBS + (j + 1))
                            dve.wait_ge(ymz_ready, g * L_JOBS + (j + 1))
                            nc.vector.tensor_tensor(modes_v[:, :, bass.ts(j, HC * KW)], ymz[:, j % 2, :, :], clip[:, :, :],
                                                    ALU.subtract).then_inc(d_ready, 1)
                            continue
                        dve.wait_ge(job_done, g * NJ + (k + 1))
                        if stage == "s1":
                            nc.vector.tensor_copy(A[:, 8 * j + 4:8 * j + 8, :], bank(k, 1)).then_inc(evac["a_dve"], 1)
                        elif stage == "s2":
                            nc.vector.tensor_copy(modes[:, :, 8 * j + 4:8 * j + 8, :],
                                                  bank(k, 1)[:, 0:4 * R2].rearrange("p (h r m) -> p r h m", h=4, r=2))\
                                .then_inc(evac["z_dve"], 1)
                        elif stage == "t":
                            nc.vector.tensor_copy(V[:, 8 * j + 4:8 * j + 8, :], bank(k, 1)).then_inc(evac["v_dve"], 1)
                        else:
                            if j >= ECH:
                                dve.wait_ge(spilled[j % ECH], g * (chunks_of(j % ECH) * 32) + (j // ECH) * 32)
                            nc.vector.tensor_copy(E[:, j % ECH, 1, :], bank(k, 1)[:, 0:I1_KW * P]).then_inc(evac["e_dve"], 1)

                    for n in range(ECH):
                        dve.wait_ge(spilled[n], (g + 1) * (chunks_of(n) * 32))

                def form_u(m, q16, n, reused):
                    dve.wait_ge(xt_in[n % UN], b * (TILES // UN * 16) + q16)
                    for k in range(CB):
                        dve.wait_ge(i2_done, m * CB + (k + 1))
                        if reused:
                            dve.wait_ge(uhi_ready, m * CB - (2 * CB - 1 - k))
                            dve.wait_ge(ulo_ready, m * CB - (2 * CB - 1 - k))
                        nc.vector.tensor_tensor(u[:, (n % 2) * CB + k, :], ps[:, k, :], xt[:, n % UN, k, :], ALU.add).then_inc(u_ready, 1)
                    for k in range(CB):
                        dve.wait_ge(uhi_ready, m * CB + (k + 1))
                        if reused:
                            dve.wait_ge(mix_done, m * CB - CB)
                        nc.vector.tensor_tensor(u_lo[:, n % 2, k, :], u[:, (n % 2) * CB + k, :], u_hi[:, n % 2, k, :].bitcast(fp32),
                                                ALU.subtract).then_inc(ulo_ready, 1)

                form_u(b * TILES, 16, 0, False)

                def tiles(q, first, last_body):
                    for n in range(UN):
                        m = (b * TILES) + (q * UN + n)
                        if not (last_body and n == UN - 1):
                            form_u(m + 1, q * 16 + (16 if n < UN - 1 else 32), n + 1, not (first and n == 0))
                        if not first or n >= 2:
                            dve.wait_ge(stored[n % 2], m * 8 - (0 if n % 2 == 0 else 8))
                        for o in range(CB):
                            dve.wait_ge(mix_done, m * CB + (o + 1))
                            nc.vector.tensor_tensor(ot[:, n % 2, o, :], ps[:, CB + o, :], xt[:, n, o, :], ALU.add).then_inc(out_ready, 1)

                tile_bodies(dve, b, tiles)
                dve.wait_ge(stored[0], (b + 1) * (TILES // 2 * 16))
                dve.wait_ge(stored[1], (b + 1) * (TILES // 2 * 16))

        @block.gpsimd
        def _(pool):
            nc.gpsimd.memset(zero[:, :], 0.0).then_inc(zeroed, 1)
            nc.gpsimd.memset(mlp_w[:, :, :], 0.0).then_inc(zeroed, 1)
            pool.wait_ge(zeroed, 2)
            with pool.Fori(0, B) as b:
                with pool.Fori(0, CB) as cb:
                    g = b * CB + cb
                    for n, w in ((0, w1r), (1, w1i), (3, w2r), (4, w2i)):
                        wk = w.rearrange("(k i) a j -> k i a j", i=2)
                        for i in range(2):
                            pool.dma_start(mlp_w[i * BS:(i + 1) * BS, n, i * BS:(i + 1) * BS], wk[cb, i, :, :]).then_inc(w_in, 16)
                    pool.dma_start(mlp_b[:, :], bias[cb, :, :]).then_inc(w_in, 16)
                    pool.wait_ge(w_in, g * 144 + 144)
                    for n in (1, 4):
                        nc.gpsimd.tensor_tensor(mlp_w[:, n + 1, :], zero[:, :], mlp_w[:, n, :], ALU.subtract).then_inc(wneg_ready, 1)
                    for j in range(L_JOBS):
                        pool.wait_ge(evac["y_act"], g * L_JOBS + (j + 1))
                        if j >= 2:
                            pool.wait_ge(d_ready, g * L_JOBS + (j - 1))
                        nc.gpsimd.tensor_tensor(ymz[:, j % 2, :, :], yt[:, j % 2, :, :], modes_v[:, :, bass.ts(j, HC * KW)],
                                                ALU.subtract).then_inc(ymz_ready, 1)
                    for j in range(I1_JOBS):
                        pool.wait_ge(evac["e_act"], g * I1_JOBS + (j + 1))
                        pool.wait_ge(evac["e_dve"], g * I1_JOBS + (j + 1))
                        for ri in range(2):
                            pool.dma_start(spill[b, :, ri * KW + I1_KW * j:ri * KW + I1_KW * (j + 1), bass.ds(cb * P, P)],
                                           E[:, j % ECH, ri, :].rearrange("p (m c) -> p m c", c=P)).then_inc(spilled[j % ECH], 16)
                    pool.wait_ge(job_done, g * NJ + NJ)

                def tiles(q, first, last_body):
                    for n in range(UN):
                        m = (b * TILES) + (q * UN + n)
                        pool.wait_ge(out_ready, m * CB + CB)
                        pool.dma_start(out_pix[b, :, :, bass.ds(q * (UN * TP) + n * TP, TP)], ot[:, n % 2, :, :]).then_inc(stored[n % 2], 16)

                for n in range(ECH):
                    pool.wait_ge(spilled[n], (b + 1) * (CB * chunks_of(n) * 32))
                nc.gpsimd.tensor_tensor(spill_mark[:, :], zero[:, 0:1], zero[:, 0:1], ALU.add).then_inc(image_spilled, 1)
                tile_bodies(pool, b, tiles)
            for n in range(2):
                pool.wait_ge(stored[n], B * TILES // 2 * 16)


def transform_constants():
    import numpy as np
    t = 2 * np.pi * np.outer(np.arange(H), np.arange(KH)) / H
    f = 2 * np.pi * np.outer(np.arange(W), np.arange(KW)) / W
    ck = np.where(np.arange(KW) == 0, 1.0, 2.0)[None, :]
    c = np.zeros((P, 772))
    c[:, 0:128] = np.concatenate([np.cos(t), -np.sin(t)], 1)
    c[:, 128:194] = np.concatenate([np.cos(f), -np.sin(f)], 1) / W
    c[:, 194:260] = np.concatenate([np.sin(f), np.cos(f)], 1) / W
    c[:, 260:388] = np.concatenate([np.cos(t).T, -np.sin(t).T], 0)
    c[:, 388:516] = np.concatenate([np.sin(t).T, np.cos(t).T], 0)
    c[0:R2, 516:644] = np.concatenate([(ck * np.cos(f)).T, -(ck * np.sin(f)).T], 0) / H
    c[:, 644:772] = np.eye(P)
    return c.astype(np.float32)


def kernel(x, L0_conv_w1_real, L0_conv_w1_imag, L0_conv_b1_real, L0_conv_b1_imag,
           L0_conv_w2_real, L0_conv_w2_imag, L0_conv_b2_real, L0_conv_b2_imag, L0_conv_fuse_w):
    import numpy as np
    import concourse.bacc as bacc
    from concourse.bass_utils import run_bass_kernel_spmd

    bias = np.stack([np.asarray(v).reshape(CB, P) for v in (L0_conv_b1_real, L0_conv_b1_imag, L0_conv_b2_real, L0_conv_b2_imag)], -1)
    arrays = {"x": x, "w1r": L0_conv_w1_real, "w1i": L0_conv_w1_imag, "w2r": L0_conv_w2_real, "w2i": L0_conv_w2_imag,
              "bias": bias, "fuse_t": np.asarray(L0_conv_fuse_w).T, "const": transform_constants()}
    arrays = {n: np.ascontiguousarray(a) for n, a in arrays.items()}
    nc = bacc.Bacc("TRN2", target_bir_lowering=False, num_devices=1)
    aps = [nc.dram_tensor(n, a.shape, mybir.dt.float32, kind="ExternalInput").ap() for n, a in arrays.items()]
    out = nc.dram_tensor("out", (B, C, H, W), mybir.dt.float32, kind="ExternalOutput").ap()
    spill = nc.dram_tensor("spill", (B, H, R2, C), mybir.dt.float32, kind="Internal").ap()
    spectral_mix(nc, *aps, out, spill)
    r = run_bass_kernel_spmd(nc, [arrays], core_ids=[0])
    return r.results[0]["out"]
```

```python
import concourse.bass as bass
from concourse import mybir
from contextlib import ExitStack

B, C, H, W = 4, 512, 128, 128
NB, BS = 8, 64
KH, KW = 64, 33
LAM = 0.01
P = 128
CB = C // P
R2 = 2 * KW
SN = 96
NCONST = R2 + 6 * P

XB = 4
XH = 8
X_JOBS = H // XH
S1_JOBS = P // 8
S2_JOBS = (KW + 7) // 8
LN = 352
L_JOBS = KH * KW // LN
T_JOBS = 5
I1_KW = 3
I1_JOBS = KW // I1_KW
EG = [(0, 4), (4, 8), (8, 11)]

TH = 4
TP = TH * W
TILES = H // TH
UN = 4

X_LIST = [("x", j) for j in range(X_JOBS)]


def forward_list(with_next_x):
    xs = iter(X_LIST)

    def some_x(n):
        return [next(xs) for _ in range(n)] if with_next_x else []

    jobs = [("s1", j) for j in range(S1_JOBS)]
    for j in range(S2_JOBS):
        jobs += [("s2", j)] + some_x(2 if j < 4 else 0)
    layers = [("l1", 0)]
    for j in range(1, L_JOBS):
        layers += [("l1", j), ("l2", j - 1)]
    layers.append(("l2", L_JOBS - 1))
    for n, job in enumerate(layers):
        jobs += [job] + some_x(1 if n % 3 == 2 else 0)
    jobs += [("t", 0), ("t", 1), ("i1", 0), ("t", 2), ("i1", 1), ("t", 3), ("i1", 2), ("t", 4), ("i1", 3)]
    for j in range(4, I1_JOBS):
        jobs += some_x(1 if j % 2 == 0 else 0) + [("i1", j)]
    return jobs + [("none", 0)] * (-len(jobs) % 4)


MIDDLE, LAST = forward_list(True), forward_list(False)
N_MIDDLE = sum(stage != "none" for stage, _ in MIDDLE)
N_IMAGE = X_JOBS + (CB - 1) * N_MIDDLE + sum(stage != "none" for stage, _ in LAST)
assert sum(job[0] == "x" for job in MIDDLE) == X_JOBS and N_IMAGE == CB * N_MIDDLE


def spectral_mix(nc, x, mlp, bias, fuse_t, const, out, spill):
    fp32 = mybir.dt.float32
    fp32r = mybir.dt.float32r
    ALU = mybir.AluOpType
    ACT = mybir.ActivationFunctionType

    x_rows = x.rearrange("b (k c) h w -> (b k) c h w", c=P)
    x_pix = x.rearrange("b (k c) h w -> b c k (h w)", c=P)
    out_pix = out.rearrange("b (k c) h w -> b c k (h w)", c=P)
    spill_r = spill.rearrange("b h m c -> b m h c")

    with ExitStack() as ctx:
        def sb(name, shape, dt=fp32):
            return ctx.enter_context(nc.sbuf_tensor(name, shape, dt))

        def sem(name):
            return ctx.enter_context(nc.semaphore(name))

        cst = sb("cst", [P, NCONST])
        f_w = cst[:, 0:SN]
        f_hr, f_hi, g_hr, g_hi, g_w, ident = [cst[:, R2 + P * n:R2 + P * (n + 1)] for n in range(6)]
        g_w = g_w[0:R2, :]
        fuse_hi = sb("fuse_hi", [P, CB, C], fp32r)
        fuse_lo = sb("fuse_lo", [P, CB, C], fp32r)

        mlp_w = sb("mlp_w", [P, 4, P])
        mlp_b = sb("mlp_b", [P, 4])
        zero = sb("zero", [P, 4, BS])
        xin = sb("xin", [P, XB, XH, W])
        big = sb("big", [P, P * P])
        xT = big[:, :].rearrange("p (h c) -> p h c", c=P)
        xt = big[:, 0:4 * CB * TP].rearrange("p (n k q) -> p n k q", n=4, k=CB)
        et = big[0:R2, 4 * CB * TP:6 * CB * TP].rearrange("p (n h c) -> p n h c", n=2, h=TH)
        ot = big[:, 6 * CB * TP:8 * CB * TP].rearrange("p (n k q) -> p n k q", n=2, k=CB)
        fuse_raw = big[:, 0:CB * C].rearrange("p (k o) -> p k o", k=CB)
        modes = sb("modes", [P, 2, KW * KH])
        modes_k = modes[:, :, :].rearrange("p g (m k) -> p g m k", k=KH)
        u = modes[:, :, :].rearrange("p g n -> p (g n)")[:, 0:2 * CB * TP].rearrange("p (n q) -> p n q", q=TP)
        hid = sb("hid", [P, 2, 2, LN])
        yt = sb("yt", [P, 2, 2, LN])
        clip = sb("clip", [P, 2, LN])
        ymz = sb("ymz", [P, 2, 2, LN])
        with nc.sbuf_tensor("fwd", [P, P * R2], fp32) as fwd:
            Bw = fwd[:, :].rearrange("p (c m) -> p c m", m=R2)
            V = fwd[:, 0:KW * P].rearrange("p (m c) -> p m c", c=P)
        u_hi = sb("u_hi", [P, 2, CB, TP], fp32r)
        u_lo = sb("u_lo", [P, 2, CB, TP], fp32r)
        sb("fwd_rest", [P, P * R2 - 4 * CB * TP])
        E = sb("E", [P, 2, KW, P])
        ps = ctx.enter_context(nc.psum_tensor("ps", [P, 8, 512], fp32))

        def bank(k, half):
            return ps[:, 2 * (k % 4) + half, :]

        def s1_out(k, half):
            return bank(k, half)[:, 0:4 * SN].rearrange("p (c m) -> p c m", m=SN)[:, :, 0:R2]

        def slot(k, p0):
            return ps[p0:p0 + 64, 2 * (k % 4):2 * (k % 4) + 2, :].rearrange("p a n -> p (a n)")

        fuse_in = sem("fuse_in")
        fuse_hi_ready, fuse_lo_ready = sem("fuse_hi_ready"), sem("fuse_lo_ready")
        zeroed = sem("zeroed")
        w_in, wneg_ready = sem("w_in"), sem("wneg_ready")
        xin_in = [sem(f"xin_in{n}") for n in range(XB)]
        job_done = sem("job_done")
        PER = {"x_act": X_JOBS, "x_dve": X_JOBS, "b_act": S1_JOBS, "b_dve": S1_JOBS, "z_act": S2_JOBS, "z_dve": S2_JOBS,
               "h_act": L_JOBS, "y_act": L_JOBS, "v_act": T_JOBS - 1, "v_dve": T_JOBS, "e_act": I1_JOBS, "e_dve": I1_JOBS}
        evac = {n: sem(n) for n in PER}
        clip_ready, ymz_ready, d_ready = sem("clip_ready"), sem("ymz_ready"), sem("d_ready")
        spilled = [sem(f"spilled{n}") for n in range(len(EG))]
        xt_in = [sem(f"xt_in{n}") for n in range(UN)]
        et_in = [sem(f"et_in{n}") for n in range(2)]
        i2_done, mix_done = sem("i2_done"), sem("mix_done")
        u_ready, uhi_ready, ulo_ready, out_ready = sem("u_ready"), sem("uhi_ready"), sem("ulo_ready"), sem("out_ready")
        stored = [sem(f"stored{n}") for n in range(2)]

        block = ctx.enter_context(nc.Block())

        def tile_bodies(eng, body):
            body(0, True, False)
            with eng.Fori(1, TILES // UN - 1) as q:
                body(q, False, False)
            body(TILES // UN - 1, False, True)

        def constants_in(eng):
            for n in range(len(EG)):
                eng.wait_ge(spilled[n], 16)

        def forward(eng, b, job, end):
            for k in range(len(X_LIST)):
                job(X_LIST, b * N_IMAGE, b * CB, k)
            end(X_LIST, b * CB)
            with eng.Fori(0, CB - 1) as cb:
                for k in range(len(MIDDLE)):
                    job(MIDDLE, b * N_IMAGE + X_JOBS + cb * N_MIDDLE, b * CB + cb, k)
                end(MIDDLE, b * CB + cb)
            for k in range(len(LAST)):
                job(LAST, b * N_IMAGE + (X_JOBS + (CB - 1) * N_MIDDLE), b * CB + (CB - 1), k)
            end(LAST, b * CB + (CB - 1))

        def x_counts(jobs):
            return 0 if jobs is X_LIST else X_JOBS

        @block.sync
        def _(sp):
            sp.dma_start(fuse_raw, fuse_t.rearrange("(k c) o -> c k o", c=P)).then_inc(fuse_in, 16)

            def load_rows(g, j):
                sp.dma_start(xin[:, j % XB, :, :], x_rows[g, :, j * XH:(j + 1) * XH, :]).then_inc(xin_in[j % XB], 16)

            with sp.Fori(0, B) as b:
                for j in range(X_JOBS):
                    if j >= XB:
                        sp.wait_ge(job_done, b * N_IMAGE + (j - XB + 1))
                    load_rows(b * CB, j)
                with sp.Fori(0, CB - 1) as cb:
                    for j in range(X_JOBS):
                        base = b * N_IMAGE + X_JOBS + cb * N_MIDDLE
                        if j < XB:
                            sp.wait_ge(job_done, base)
                        else:
                            sp.wait_ge(job_done, base + (MIDDLE.index(("x", j - XB)) + 1))
                        load_rows(b * CB + cb + 1, j)
                for n in range(len(EG)):
                    sp.wait_ge(spilled[n], b * (CB * 32) + (CB * 32 + 16))

                def load_tiles(q, first, last):
                    for n in range(UN):
                        m = (b * TILES) + (q * UN + n)
                        if not first:
                            sp.wait_ge(out_ready, m * CB - (UN - 1) * CB)
                        sp.dma_start(xt[:, n, :, :], x_pix[b, :, :, bass.ds(q * (UN * TP) + n * TP, TP)]).then_inc(xt_in[n], 16)
                        if not first or n >= 2:
                            sp.wait_ge(i2_done, m * CB - CB)
                        sp.dma_start(et[:, n % 2, :, :], spill_r[b, :, bass.ds(q * (UN * TH) + n * TH, TH), :]).then_inc(et_in[n % 2], 16)

                tile_bodies(sp, load_tiles)

        @block.tensor
        def _(pe):
            mm = nc.tensor.matmul

            def taken(stage, j, x_before=0):
                n = j + 1
                return {"x": {"x_act": x_before + n, "x_dve": x_before + n}, "s1": {"b_act": n, "b_dve": n},
                        "s2": {"z_act": n, "z_dve": n}, "l1": {"h_act": n}, "l2": {"y_act": n},
                        "t": {"v_act": min(n, T_JOBS - 1), "v_dve": n}, "i1": {"e_act": n, "e_dve": n}, "none": {}}[stage]

            def forward_end(jobs, g):
                if jobs is not X_LIST:
                    pe.wait_ge(evac["e_act"], g * I1_JOBS + I1_JOBS)
                    pe.wait_ge(evac["e_dve"], g * I1_JOBS + I1_JOBS)

            def forward_job(jobs, base, g, k):
                stage, j = jobs[k]
                if stage == "none":
                    return

                def wait_for(inputs):
                    before = taken(*jobs[k - 4], x_counts(jobs)) if k >= 4 else {}
                    for name in {**before, **inputs}:
                        pe.wait_ge(evac[name], g * PER[name] + max(before.get(name, 0), inputs.get(name, 0)))

                if stage == "x":
                    wait_for({})
                    pe.wait_ge(xin_in[j % XB], (g * X_JOBS + x_counts(jobs)) * (16 // XB) + (j // XB + 1) * 16)
                    for i in range(XH):
                        last = nc.tensor.transpose(bank(k, i // 4)[:, (i % 4) * P:(i % 4 + 1) * P], xin[:, j % XB, i, :], ident)
                elif stage == "s1":
                    wait_for({"x_act": X_JOBS, "x_dve": X_JOBS} if j == 0 else {})
                    for i in range(8):
                        last = mm(bank(k, i // 4)[:, (i % 4) * SN:(i % 4 + 1) * SN], xT[:, :, 8 * j + i], f_w, start=True, stop=True)
                elif stage == "s2":
                    wait_for(taken("s1", S1_JOBS - 1))
                    for i in range(min(8, KW - 8 * j)):
                        kw = 8 * j + i
                        o = bank(k, i // 4)[:, (i % 4) * P:(i % 4 + 1) * P]
                        mm(o, Bw[:, :, kw], f_hr, start=True, stop=False)
                        last = mm(o, Bw[:, :, KW + kw], f_hi, start=False, stop=True)
                elif stage == "l1":
                    wait_for(taken("s2", ((j + 1) * LN - 1) // KH // 8))
                    if j == 0:
                        pe.wait_ge(wneg_ready, g + 1)
                    for n in range(2):
                        last = mm(bank(k, n)[:, 0:LN], mlp_w[:, n, :], modes[:, n, j * LN:(j + 1) * LN], start=True, stop=True)
                elif stage == "l2":
                    wait_for(taken("l1", j))
                    for n in range(2):
                        last = mm(bank(k, n)[:, 0:LN], mlp_w[:, 2 + n, :], hid[:, j % 2, n, :], start=True, stop=True)
                elif stage == "t":
                    wait_for({})
                    if j == 0:
                        pe.wait_ge(d_ready, g * L_JOBS + L_JOBS)
                    cols = [(j % 2, 16 * (j // 2) + 2 * i) for i in range(8)] if j < T_JOBS - 1 else [(0, KW - 2), (1, KW - 2)]
                    for i, (n, kw) in enumerate(cols):
                        last = nc.tensor.transpose(bank(k, i // 4)[:, (i % 4) * P:(i % 4 + 1) * P],
                                                   modes[:, n, kw * KH:(kw + 2) * KH], ident)
                else:
                    kw = I1_KW * j + I1_KW - 1
                    wait_for(taken("t", T_JOBS - 1 if kw == KW - 1 else 2 * (kw // 16) + 1))
                    v = V[:, I1_KW * j:I1_KW * (j + 1), :]
                    mm(bank(k, 0)[:, 0:I1_KW * P], g_hr, v, start=True, stop=True)
                    last = mm(bank(k, 1)[:, 0:I1_KW * P], g_hi, v, start=True, stop=True)
                last.then_inc(job_done, 1)

            constants_in(pe)
            pe.wait_ge(fuse_hi_ready, 1)
            pe.wait_ge(fuse_lo_ready, 1)
            with pe.Fori(0, B) as b:
                forward(pe, b, forward_job, forward_end)

                def inverse_w(m, n, first):
                    pe.wait_ge(et_in[n % 2], m * 8 + (16 if n % 2 == 0 else 8))
                    for k in range(CB):
                        if not first:
                            pe.wait_ge(u_ready, m * CB - (CB - 1 - k))
                        for h in range(TH):
                            last = mm(ps[:, k, h * W:(h + 1) * W], et[:, n % 2, h, k * P:(k + 1) * P], g_w, start=True, stop=True)
                        last.then_inc(i2_done, 1)

                def mix_tiles(q, first, last_body):
                    for n in range(UN):
                        m = (b * TILES) + (q * UN + n)
                        if not (last_body and n == UN - 1):
                            inverse_w(m + 1, n + 1, False)
                        for o in range(CB):
                            if not (first and n == 0):
                                pe.wait_ge(out_ready, m * CB - (CB - 1 - o))
                            for k in range(CB):
                                if o == 0:
                                    pe.wait_ge(uhi_ready, m * CB + (k + 1))
                                    pe.wait_ge(ulo_ready, m * CB + (k + 1))
                                w_hi, w_lo = fuse_hi[:, k, o * P:(o + 1) * P], fuse_lo[:, k, o * P:(o + 1) * P]
                                mm(ps[:, CB + o, :], w_hi, u_hi[:, n % 2, k, :], start=(k == 0), stop=False)
                                mm(ps[:, CB + o, :], w_hi, u_lo[:, n % 2, k, :], start=False, stop=False)
                                last = mm(ps[:, CB + o, :], w_lo, u_hi[:, n % 2, k, :], start=False, stop=(k == CB - 1))
                            last.then_inc(mix_done, 1)

                inverse_w(b * TILES, 0, True)
                tile_bodies(pe, mix_tiles)
                pe.wait_ge(out_ready, (b + 1) * (TILES * CB))

        @block.scalar
        def _(act):
            copy = nc.scalar.activation

            def forward_job(jobs, base, g, k):
                stage, j = jobs[k]
                if stage == "none":
                    return
                act.wait_ge(job_done, base + (k + 1))
                if stage == "x":
                    copy(xT[:, XH * j:XH * j + 4, :], bank(k, 0), ACT.Copy).then_inc(evac["x_act"], 1)
                elif stage == "s1":
                    copy(Bw[:, 8 * j:8 * j + 4, :], s1_out(k, 0), ACT.Copy).then_inc(evac["b_act"], 1)
                elif stage == "s2":
                    z = slot(k, 0).rearrange("p (m r h) -> p r m h", r=2, h=KH)
                    n = min(8, KW - 8 * j)
                    copy(modes_k[0:64, 0, 8 * j:8 * j + n, :], z[:, 0, 0:n, :], ACT.Copy)
                    copy(modes_k[64:128, 0, 8 * j:8 * j + n, :], z[:, 1, 0:n, :], ACT.Copy).then_inc(evac["z_act"], 1)
                elif stage == "l1":
                    copy(hid[:, j % 2, 0, :], bank(k, 0)[:, 0:LN], ACT.Gelu, bias=mlp_b[:, 0:1])
                    copy(hid[:, j % 2, 1, :], bank(k, 1)[:, 0:LN], ACT.Gelu, bias=mlp_b[:, 1:2]).then_inc(evac["h_act"], 1)
                elif stage == "l2":
                    if j >= 2:
                        act.wait_ge(clip_ready, g * L_JOBS + (j - 1))
                        act.wait_ge(ymz_ready, g * L_JOBS + (j - 1))
                    copy(yt[:, j % 2, 0, :], bank(k, 0)[:, 0:LN], ACT.Identity, bias=mlp_b[:, 2:3])
                    copy(yt[:, j % 2, 1, :], bank(k, 1)[:, 0:LN], ACT.Identity, bias=mlp_b[:, 3:4]).then_inc(evac["y_act"], 1)
                elif stage == "t":
                    if j < T_JOBS - 1:
                        m, n = 16 * (j // 2), BS * (j % 2)
                        d = slot(k, 0).rearrange("p (i r c) -> p i r c", r=2, c=BS)
                        copy(V[0:64, m:m + 16:2, n:n + BS], d[:, :, 0, :], ACT.Copy)
                        copy(V[64:128, m:m + 16:2, n:n + BS], d[:, :, 1, :], ACT.Copy).then_inc(evac["v_act"], 1)
                else:
                    for n, (lo, _) in enumerate(EG):
                        if j == lo:
                            act.wait_ge(spilled[n], g * 32 + 16)
                    copy(E[:, 0, I1_KW * j:I1_KW * (j + 1), :], bank(k, 0)[:, 0:I1_KW * P], ACT.Copy).then_inc(evac["e_act"], 1)

            act.wait_ge(fuse_in, 16)
            copy(fuse_hi[:, :, :], fuse_raw, ACT.Copy).then_inc(fuse_hi_ready, 1)
            act.wait_ge(fuse_lo_ready, 1)
            with act.Fori(0, B) as b:
                forward(act, b, forward_job, lambda jobs, g: None)

                def upper_u(m, n, reused):
                    for k in range(CB):
                        act.wait_ge(u_ready, m * CB + (k + 1))
                        if reused:
                            act.wait_ge(mix_done, m * CB - CB)
                        copy(u_hi[:, n % 2, k, :], u[:, (n % 2) * CB + k, :], ACT.Copy).then_inc(uhi_ready, 1)

                upper_u(b * TILES, 0, False)

                def tiles(q, first, last_body):
                    for n in range(UN):
                        m = (b * TILES) + (q * UN + n)
                        if not (last_body and n == UN - 1):
                            upper_u(m + 1, n + 1, not (first and n == 0))

                tile_bodies(act, tiles)
                act.wait_ge(stored[0], (b + 1) * (TILES // 2 * 16))
                act.wait_ge(stored[1], (b + 1) * (TILES // 2 * 16))
                act.wait_ge(out_ready, (b + 1) * (TILES * CB))

        @block.vector
        def _(dve):
            copy = nc.vector.tensor_copy

            def forward_job(jobs, base, g, k):
                stage, j = jobs[k]
                if stage in ("none", "l1"):
                    return
                if stage == "l2":
                    dve.wait_ge(evac["y_act"], g * L_JOBS + (j + 1))
                    if j:
                        dve.wait_ge(d_ready, g * L_JOBS + j)
                    nc.vector.tensor_scalar(clip[:, :, :], yt[:, j % 2, :, :], -LAM, LAM, ALU.max, ALU.min).then_inc(clip_ready, 1)
                    dve.wait_ge(clip_ready, g * L_JOBS + (j + 1))
                    dve.wait_ge(ymz_ready, g * L_JOBS + (j + 1))
                    nc.vector.tensor_tensor(modes[:, :, j * LN:(j + 1) * LN], ymz[:, j % 2, :, :], clip[:, :, :],
                                            ALU.subtract).then_inc(d_ready, 1)
                    return
                dve.wait_ge(job_done, base + (k + 1))
                if stage == "x":
                    copy(xT[:, XH * j + 4:XH * j + 8, :], bank(k, 1)).then_inc(evac["x_dve"], 1)
                elif stage == "s1":
                    copy(Bw[:, 8 * j + 4:8 * j + 8, :], s1_out(k, 1)).then_inc(evac["b_dve"], 1)
                elif stage == "s2":
                    z = slot(k, 64).rearrange("p (m r h) -> p r m h", r=2, h=KH)
                    n = min(8, KW - 8 * j)
                    copy(modes_k[0:64, 1, 8 * j:8 * j + n, :], z[:, 0, 0:n, :])
                    copy(modes_k[64:128, 1, 8 * j:8 * j + n, :], z[:, 1, 0:n, :]).then_inc(evac["z_dve"], 1)
                elif stage == "t":
                    d = slot(k, 64).rearrange("p (i r c) -> p i r c", r=2, c=BS)
                    if j < T_JOBS - 1:
                        m, n = 16 * (j // 2), BS * (j % 2)
                        copy(V[0:64, m + 1:m + 16:2, n:n + BS], d[:, :, 0, :])
                        copy(V[64:128, m + 1:m + 16:2, n:n + BS], d[:, :, 1, :]).then_inc(evac["v_dve"], 1)
                    else:
                        v = V[:, KW - 1, :].rearrange("p (i c) -> p i c", c=BS)
                        copy(v[0:64], d[:, 0:2, 0, :])
                        copy(v[64:128], d[:, 0:2, 1, :]).then_inc(evac["v_dve"], 1)
                else:
                    for n, (lo, _) in enumerate(EG):
                        if j == lo:
                            dve.wait_ge(spilled[n], g * 32 + 16)
                    copy(E[:, 1, I1_KW * j:I1_KW * (j + 1), :], bank(k, 1)[:, 0:I1_KW * P]).then_inc(evac["e_dve"], 1)

            dve.wait_ge(fuse_hi_ready, 1)
            nc.vector.tensor_tensor(fuse_lo[:, :, :], fuse_raw, fuse_hi[:, :, :].bitcast(fp32), ALU.subtract).then_inc(fuse_lo_ready, 1)
            dve.wait_ge(fuse_lo_ready, 1)
            with dve.Fori(0, B) as b:
                forward(dve, b, forward_job, lambda jobs, g: None)

                def form_u(m, q16, n, reused):
                    dve.wait_ge(xt_in[n % UN], b * (TILES // UN * 16) + q16)
                    for k in range(CB):
                        dve.wait_ge(i2_done, m * CB + (k + 1))
                        if reused:
                            dve.wait_ge(uhi_ready, m * CB - (2 * CB - 1 - k))
                            dve.wait_ge(ulo_ready, m * CB - (2 * CB - 1 - k))
                        nc.vector.tensor_tensor(u[:, (n % 2) * CB + k, :], ps[:, k, :], xt[:, n % UN, k, :], ALU.add).then_inc(u_ready, 1)
                    for k in range(CB):
                        dve.wait_ge(uhi_ready, m * CB + (k + 1))
                        if reused:
                            dve.wait_ge(mix_done, m * CB - CB)
                        nc.vector.tensor_tensor(u_lo[:, n % 2, k, :], u[:, (n % 2) * CB + k, :], u_hi[:, n % 2, k, :].bitcast(fp32),
                                                ALU.subtract).then_inc(ulo_ready, 1)

                form_u(b * TILES, 16, 0, False)

                def tiles(q, first, last_body):
                    for n in range(UN):
                        m = (b * TILES) + (q * UN + n)
                        if not (last_body and n == UN - 1):
                            form_u(m + 1, q * 16 + (16 if n < UN - 1 else 32), n + 1, not (first and n == 0))
                        if not first or n >= 2:
                            dve.wait_ge(stored[n % 2], m * 8 - (0 if n % 2 == 0 else 8))
                        for o in range(CB):
                            dve.wait_ge(mix_done, m * CB + (o + 1))
                            nc.vector.tensor_tensor(ot[:, n % 2, o, :], ps[:, CB + o, :], xt[:, n, o, :], ALU.add).then_inc(out_ready, 1)

                tile_bodies(dve, tiles)
                dve.wait_ge(stored[0], (b + 1) * (TILES // 2 * 16))
                dve.wait_ge(stored[1], (b + 1) * (TILES // 2 * 16))

        @block.gpsimd
        def _(pool):
            for n in range(len(EG)):
                part = slice(n * NCONST // len(EG), (n + 1) * NCONST // len(EG))
                pool.dma_start(cst[:, part], const[:, part]).then_inc(spilled[n], 16)
            nc.gpsimd.memset(zero[:, :, :], 0.0).then_inc(zeroed, 1)
            pool.wait_ge(zeroed, 1)

            with pool.Fori(0, B) as b:
                with pool.Fori(0, CB) as cb:
                    g = b * CB + cb
                    pool.dma_start(mlp_w[:, :, :], mlp[cb, :, :, :]).then_inc(w_in, 16)
                    pool.dma_start(mlp_b[:, :], bias[cb, :, :]).then_inc(w_in, 16)
                    pool.wait_ge(w_in, g * 32 + 32)
                    nc.gpsimd.tensor_tensor(mlp_w[64:128, :, 0:BS], zero[64:128, :, :], mlp_w[64:128, :, 0:BS],
                                            ALU.subtract).then_inc(wneg_ready, 1)
                    for j in range(L_JOBS):
                        pool.wait_ge(evac["y_act"], g * L_JOBS + (j + 1))
                        if j >= 2:
                            pool.wait_ge(d_ready, g * L_JOBS + (j - 1))
                        nc.gpsimd.tensor_tensor(ymz[:, j % 2, :, :], yt[:, j % 2, :, :], modes[:, :, j * LN:(j + 1) * LN],
                                                ALU.subtract).then_inc(ymz_ready, 1)
                    for n, (lo, hi) in enumerate(EG):
                        pool.wait_ge(evac["e_act"], g * I1_JOBS + hi)
                        pool.wait_ge(evac["e_dve"], g * I1_JOBS + hi)
                        for ri in range(2):
                            pool.dma_start(spill[b, :, ri * KW + I1_KW * lo:ri * KW + I1_KW * hi, bass.ds(cb * P, P)],
                                           E[:, ri, I1_KW * lo:I1_KW * hi, :]).then_inc(spilled[n], 16)

                def tiles(q, first, last_body):
                    for n in range(UN):
                        m = (b * TILES) + (q * UN + n)
                        pool.wait_ge(out_ready, m * CB + CB)
                        pool.dma_start(out_pix[b, :, :, bass.ds(q * (UN * TP) + n * TP, TP)], ot[:, n % 2, :, :]).then_inc(stored[n % 2], 16)

                tile_bodies(pool, tiles)
            for n in range(2):
                pool.wait_ge(stored[n], B * TILES // 2 * 16)


def transform_constants():
    import numpy as np
    t = 2 * np.pi * np.outer(np.arange(H), np.arange(KH)) / H
    f = 2 * np.pi * np.outer(np.arange(W), np.arange(KW)) / W
    ck = np.where(np.arange(KW) == 0, 1.0, 2.0)[None, :]
    g_w = np.zeros((P, W))
    g_w[0:R2] = np.concatenate([(ck * np.cos(f)).T, -(ck * np.sin(f)).T], 0) / H
    parts = [np.concatenate([np.cos(f), -np.sin(f)], 1) / W,
             np.concatenate([np.cos(t), -np.sin(t)], 1), np.concatenate([np.sin(t), np.cos(t)], 1),
             np.concatenate([np.cos(t).T, -np.sin(t).T], 0), np.concatenate([np.sin(t).T, np.cos(t).T], 0),
             g_w, np.eye(P)]
    return np.concatenate(parts, 1).astype(np.float32)


def kernel(x, L0_conv_w1_real, L0_conv_w1_imag, L0_conv_b1_real, L0_conv_b1_imag,
           L0_conv_w2_real, L0_conv_w2_imag, L0_conv_b2_real, L0_conv_b2_imag, L0_conv_fuse_w):
    import numpy as np
    import concourse.bacc as bacc
    from concourse.bass_utils import run_bass_kernel_spmd

    def stacked(wr, wi):
        wr, wi = np.asarray(wr), np.asarray(wi)
        return np.concatenate([np.concatenate([wr, wi], 2), np.concatenate([wi, wr], 2)], 1)

    layers = [stacked(L0_conv_w1_real, L0_conv_w1_imag), stacked(L0_conv_w2_real, L0_conv_w2_imag)]
    mlp = np.stack([w.reshape(CB, 2, P, P) for w in layers], 1).transpose(0, 3, 1, 2, 4).reshape(CB, P, 4, P)
    biases = [np.concatenate([np.asarray(r), np.asarray(i)], 1) for r, i in
              ((L0_conv_b1_real, L0_conv_b1_imag), (L0_conv_b2_real, L0_conv_b2_imag))]
    bias = np.stack([v.reshape(CB, 2, P) for v in biases], 1).transpose(0, 3, 1, 2).reshape(CB, P, 4)
    arrays = {"x": x, "mlp": mlp, "bias": bias, "fuse_t": np.asarray(L0_conv_fuse_w).T, "const": transform_constants()}
    arrays = {n: np.ascontiguousarray(a) for n, a in arrays.items()}
    nc = bacc.Bacc("TRN2", target_bir_lowering=False, num_devices=1)
    aps = [nc.dram_tensor(n, a.shape, mybir.dt.float32, kind="ExternalInput").ap() for n, a in arrays.items()]
    out = nc.dram_tensor("out", (B, C, H, W), mybir.dt.float32, kind="ExternalOutput").ap()
    spill = nc.dram_tensor("spill", (B, H, R2, C), mybir.dt.float32, kind="Internal").ap()
    spectral_mix(nc, *aps, out, spill)
    r = run_bass_kernel_spmd(nc, [arrays], core_ids=[0])
    return r.results[0]["out"]
```

```python
import concourse.bass as bass
from concourse import mybir
from contextlib import ExitStack

B, C, H, W = 4, 512, 128, 128
NB, BS = 8, 64
KH, KW = 64, 33
LAM = 0.01
P = 128
CB = C // P
R2 = 2 * KW
SN = 96
NCONST = R2 + 6 * P

XB = 4
XH = 8
XE = 8
X_JOBS = H // XH
S1_JOBS = P // 8
S2_JOBS = (KW + 7) // 8
LN = 352
L_JOBS = KH * KW // LN
T_JOBS = 5
I1_KW = 3
I1_JOBS = KW // I1_KW
EG = [(0, 4), (4, 8), (8, 10), (10, 11)]

TH = 4
TP = TH * W
TILES = H // TH
UN = 4

X_LIST = [("x", j) for j in range(X_JOBS)]


def forward_list(with_next_x):
    xs = iter(X_LIST)

    def some_x(n):
        return [next(xs) for _ in range(n)] if with_next_x else []

    jobs = [("s1", j) for j in range(S1_JOBS)]
    jobs += some_x(1)
    for j in range(S2_JOBS):
        jobs += [("s2", j)] + some_x(1 if j == 0 else 2 if j < 4 else 0)
    layers = [("l1", 0)]
    for j in range(1, L_JOBS):
        layers += [("l1", j), ("l2", j - 1)]
    layers.append(("l2", L_JOBS - 1))
    for n, job in enumerate(layers):
        jobs += [job] + some_x(1 if n % 3 == 1 else 0)
        if job == ("l1", L_JOBS - 1):
            jobs += [("t", 0), ("t", 1)]
    jobs += [("i1", 0), ("i1", 1), ("i1", 2), ("t", 2), ("t", 3), ("i1", 3), ("i1", 4), ("t", 4)]
    for j in range(5, I1_JOBS):
        jobs += some_x(1 if j < 9 else 0) + [("i1", j)]
    for n in range(-len(jobs) % 4):
        jobs.insert(jobs.index(("s2", n)) + 1, ("none", 0))
    return jobs


MIDDLE, LAST = forward_list(True), forward_list(False)


def jobs_up_to(jobs, k):
    return sum(stage != "none" for stage, _ in jobs[:k + 1])


BEFORE = [[job for job in MIDDLE[n::4] if job[0] != "none"][-1] for n in range(4)]
assert all(stage in ("i1", "x") for stage, _ in BEFORE)
N_MIDDLE = jobs_up_to(MIDDLE, len(MIDDLE))
N_IMAGE = X_JOBS + (CB - 1) * N_MIDDLE + jobs_up_to(LAST, len(LAST))
assert sum(job[0] == "x" for job in MIDDLE) == X_JOBS and N_IMAGE == CB * N_MIDDLE


def spectral_mix(nc, x, mlp, bias, fuse_t, const, out, spill):
    fp32 = mybir.dt.float32
    fp32r = mybir.dt.float32r
    ALU = mybir.AluOpType
    ACT = mybir.ActivationFunctionType

    x_rows = x.rearrange("b (k c) h w -> (b k) c h w", c=P)
    x_pix = x.rearrange("b (k c) h w -> b c k (h w)", c=P)
    out_pix = out.rearrange("b (k c) h w -> b c k (h w)", c=P)
    spill_r = spill.rearrange("b h m c -> b m h c")

    with ExitStack() as ctx:
        def sb(name, shape, dt=fp32):
            return ctx.enter_context(nc.sbuf_tensor(name, shape, dt))

        def sem(name):
            return ctx.enter_context(nc.semaphore(name))

        cst = sb("cst", [P, NCONST])
        f_w = cst[:, 0:SN]
        f_hr, f_hi, g_hr, g_hi, g_w, ident = [cst[:, R2 + P * n:R2 + P * (n + 1)] for n in range(6)]
        g_w = g_w[0:R2, :]
        fuse_hi = sb("fuse_hi", [P, CB, C], fp32r)
        fuse_lo = sb("fuse_lo", [P, CB, C], fp32r)

        mlp_w = sb("mlp_w", [P, 4, P])
        mlp_b = sb("mlp_b", [P, 4])
        zero = sb("zero", [P, 4, BS])
        xin = sb("xin", [P, XB, XH, W])
        big = sb("big", [P, P * P])
        xT = big[:, :].rearrange("p (h c) -> p h c", c=P)
        xt = big[:, 0:4 * CB * TP].rearrange("p (n k q) -> p n k q", n=4, k=CB)
        et = big[0:R2, 4 * CB * TP:6 * CB * TP].rearrange("p (n h c) -> p n h c", n=2, h=TH)
        ot = big[:, 6 * CB * TP:8 * CB * TP].rearrange("p (n k q) -> p n k q", n=2, k=CB)
        fuse_raw = big[:, 0:CB * C].rearrange("p (k o) -> p k o", k=CB)
        modes = sb("modes", [P, 2, KW * KH])
        modes_k = modes[:, :, :].rearrange("p g (m k) -> p g m k", k=KH)
        u = modes[:, :, :].rearrange("p g n -> p (g n)")[:, 0:2 * CB * TP].rearrange("p (n q) -> p n q", q=TP)
        hid = sb("hid", [P, 2, 2, LN])
        yt = sb("yt", [P, 2, 2, LN])
        clip = sb("clip", [P, 2, LN])
        ymz = sb("ymz", [P, 2, 2, LN])
        with nc.sbuf_tensor("fwd", [P, P * R2], fp32) as fwd:
            Bw = fwd[:, :].rearrange("p (c m) -> p c m", m=R2)
            V = fwd[:, 0:KW * P].rearrange("p (m c) -> p m c", c=P)
        u_hi = sb("u_hi", [P, 2, CB, TP], fp32r)
        u_lo = sb("u_lo", [P, 2, CB, TP], fp32r)
        sb("fwd_rest", [P, P * R2 - 4 * CB * TP])
        E = sb("E", [P, 2, KW, P])
        xearly = E[:, :, :, :].rearrange("p r m c -> p (r m c)")[:, 0:XE * XH * W].rearrange("p (n h w) -> p n h w", n=XE, h=XH)
        ps = ctx.enter_context(nc.psum_tensor("ps", [P, 8, 512], fp32))

        def bank(k, half):
            return ps[:, 2 * (k % 4) + half, :]

        def s1_out(k, half):
            return bank(k, half)[:, 0:4 * SN].rearrange("p (c m) -> p c m", m=SN)[:, :, 0:R2]

        def slot(k, p0):
            return ps[p0:p0 + 64, 2 * (k % 4):2 * (k % 4) + 2, :].rearrange("p a n -> p (a n)")

        fuse_in = sem("fuse_in")
        fuse_hi_ready, fuse_lo_ready = sem("fuse_hi_ready"), sem("fuse_lo_ready")
        zeroed = sem("zeroed")
        w_in, wneg_ready = sem("w_in"), sem("wneg_ready")
        xin_in = [sem(f"xin_in{n}") for n in range(XB)]
        xearly_in = [sem(f"xearly_in{n}") for n in range(XE)]
        job_done = sem("job_done")
        PER = {"x_act": X_JOBS, "x_dve": X_JOBS, "b_act": S1_JOBS, "b_dve": S1_JOBS, "z_act": S2_JOBS, "z_dve": S2_JOBS,
               "h_act": L_JOBS, "y_act": L_JOBS, "v_act": T_JOBS - 1, "v_dve": T_JOBS, "e_act": I1_JOBS, "e_dve": I1_JOBS}
        evac = {n: sem(n) for n in PER}
        CREDIT = {"e_act": I1_JOBS, "e_dve": I1_JOBS}
        clip_ready, ymz_ready, d_ready = sem("clip_ready"), sem("ymz_ready"), sem("d_ready")
        spilled = [sem(f"spilled{n}") for n in range(len(EG))]
        xt_in = [sem(f"xt_in{n}") for n in range(UN)]
        et_in = [sem(f"et_in{n}") for n in range(2)]
        et_first_in = sem("et_first_in")
        i2_done, mix_done = sem("i2_done"), sem("mix_done")
        u_ready, uhi_ready, ulo_ready, out_ready = sem("u_ready"), sem("uhi_ready"), sem("ulo_ready"), sem("out_ready")
        stored = [sem(f"stored{n}") for n in range(2)]

        block = ctx.enter_context(nc.Block())

        def tile_bodies(eng, body):
            body(0, True, False)
            with eng.Fori(1, TILES // UN - 1) as q:
                body(q, False, False)
            body(TILES // UN - 1, False, True)

        OT = 6 * CB * TP

        def output_stored(eng, b):
            for n in range(2):
                eng.wait_ge(stored[n], b * (TILES // 2 * 16) + 16)

        def constants_in(eng):
            for signal in spilled + stored:
                eng.wait_ge(signal, 16)

        def forward(eng, b, job):
            for k in range(len(X_LIST)):
                job(X_LIST, b * N_IMAGE, b, 0, k)
            with eng.Fori(0, CB - 1) as cb:
                for k in range(len(MIDDLE)):
                    job(MIDDLE, b * N_IMAGE + X_JOBS + cb * N_MIDDLE, b, cb, k)
            for k in range(len(LAST)):
                job(LAST, b * N_IMAGE + (X_JOBS + (CB - 1) * N_MIDDLE), b, CB - 1, k)

        X_FIRST = X_JOBS - XE
        X_IMAGE = X_FIRST + (CB - 1) * X_JOBS

        def x_counts(jobs):
            return 0 if jobs is X_LIST else X_JOBS

        @block.sync
        def _(sp):
            sp.dma_start(fuse_raw, fuse_t.rearrange("(k c) o -> c k o", c=P)).then_inc(fuse_in, 16)

            def load_rows(g, j):
                sp.dma_start(xin[:, j % XB, :, :], x_rows[g, :, j * XH:(j + 1) * XH, :]).then_inc(xin_in[j % XB], 16)

            with sp.Fori(0, B) as b:
                for j in range(XB):
                    load_rows(b * CB, j)
                sp.wait_ge(fuse_in, 16)
                for n in range(XE):
                    j = XB + n
                    sp.dma_start(xearly[:, n, :, :], x_rows[b * CB, :, j * XH:(j + 1) * XH, :]).then_inc(xearly_in[n], 16)
                for j in range(XB + XE, X_JOBS):
                    sp.wait_ge(job_done, b * N_IMAGE + (j - XB - XE + 1))
                    load_rows(b * CB, j)
                with sp.Fori(0, CB - 1) as cb:
                    for j in range(X_JOBS):
                        base = b * N_IMAGE + X_JOBS + cb * N_MIDDLE
                        if j < XB:
                            sp.wait_ge(job_done, base)
                        else:
                            sp.wait_ge(job_done, base + jobs_up_to(MIDDLE, MIDDLE.index(("x", j - XB))))
                        load_rows(b * CB + cb + 1, j)
                sp.wait_ge(job_done, b * N_IMAGE + (X_JOBS + (CB - 1) * N_MIDDLE + S1_JOBS))
                for n in range(UN):
                    sp.dma_start(xt[:, n, :, :], x_pix[b, :, :, n * TP:(n + 1) * TP]).then_inc(xt_in[n], 16)
                for n in range(len(EG)):
                    sp.wait_ge(spilled[n], b * (CB * 32) + ((CB - 1) * 32 + 16))
                sp.dma_start(et[:, 0, :, 0:C - P], spill_r[b, :, 0:TH, 0:C - P]).then_inc(et_first_in, 16)
                for n in range(len(EG)):
                    sp.wait_ge(spilled[n], b * (CB * 32) + (CB * 32 + 16))

                def load_tiles(q, first, last):
                    for n in range(UN):
                        m = (b * TILES) + (q * UN + n)
                        if not first:
                            sp.wait_ge(out_ready, m * CB - (UN - 1) * CB)
                            sp.dma_start(xt[:, n, :, :], x_pix[b, :, :, bass.ds(q * (UN * TP) + n * TP, TP)]).then_inc(xt_in[n], 16)
                        if not first or n >= 2:
                            sp.wait_ge(i2_done, m * CB - CB)
                        c = C - P if first and n == 0 else 0
                        sp.dma_start(et[:, n % 2, :, c:C], spill_r[b, :, bass.ds(q * (UN * TH) + n * TH, TH), c:C]).then_inc(et_in[n % 2], 16)

                tile_bodies(sp, load_tiles)

        @block.tensor
        def _(pe):
            mm = nc.tensor.matmul

            def taken(stage, j, x_before=0):
                n = j + 1
                return {"x": {"x_act": x_before + n, "x_dve": x_before + n}, "s1": {"b_act": n, "b_dve": n},
                        "s2": {"z_act": n, "z_dve": n}, "l1": {"h_act": n}, "l2": {"y_act": n},
                        "t": {"v_act": min(n, T_JOBS - 1), "v_dve": n}, "i1": {"e_act": n, "e_dve": n}, "none": {}}[stage]

            def forward_job(jobs, base, b, cb, k):
                stage, j = jobs[k]
                g = b * CB + cb
                if stage == "none":
                    return

                def wait_for(inputs):
                    before = {}
                    if k >= 4:
                        before = taken(*next(jobs[i] for i in range(k - 4, -1, -4) if jobs[i][0] != "none"), x_counts(jobs))
                    elif jobs is not X_LIST and BEFORE[k][0] == "i1":
                        before = {name: n - I1_JOBS for name, n in taken(*BEFORE[k]).items()}
                    for name in {**before, **inputs}:
                        n = max(v[name] for v in (before, inputs) if name in v)
                        pe.wait_ge(evac[name], g * PER[name] + (CREDIT.get(name, 0) + n))

                if stage == "x":
                    wait_for({})
                    rows = xin[:, j % XB, :, :]
                    in_images_before = b * (X_IMAGE // XB * 16)
                    if jobs is not X_LIST:
                        in_lists_before = cb * (X_JOBS // XB * 16) + X_FIRST // XB * 16
                        pe.wait_ge(xin_in[j % XB], in_images_before + in_lists_before + (j // XB + 1) * 16)
                    elif j < XB:
                        pe.wait_ge(xin_in[j % XB], in_images_before + 16)
                    elif j < XB + XE:
                        rows = xearly[:, j - XB, :, :]
                        pe.wait_ge(xearly_in[j - XB], b * 16 + 16)
                    else:
                        pe.wait_ge(xin_in[j % XB], in_images_before + ((j - XE) // XB + 1) * 16)
                    for i in range(XH):
                        last = nc.tensor.transpose(bank(k, i // 4)[:, (i % 4) * P:(i % 4 + 1) * P], rows[:, i, :], ident)
                elif stage == "s1":
                    wait_for({"x_act": X_JOBS, "x_dve": X_JOBS} if j == 0 else {})
                    for i in range(8):
                        last = mm(bank(k, i // 4)[:, (i % 4) * SN:(i % 4 + 1) * SN], xT[:, :, 8 * j + i], f_w, start=True, stop=True)
                elif stage == "s2":
                    wait_for(taken("s1", S1_JOBS - 1))
                    for i in range(min(8, KW - 8 * j)):
                        kw = 8 * j + i
                        o = bank(k, i // 4)[:, (i % 4) * P:(i % 4 + 1) * P]
                        mm(o, Bw[:, :, kw], f_hr, start=True, stop=False)
                        last = mm(o, Bw[:, :, KW + kw], f_hi, start=False, stop=True)
                elif stage == "l1":
                    wait_for(taken("s2", ((j + 1) * LN - 1) // KH // 8))
                    if j == 0:
                        pe.wait_ge(wneg_ready, g + 1)
                    for n in range(2):
                        last = mm(bank(k, n)[:, 0:LN], mlp_w[:, n, :], modes[:, n, j * LN:(j + 1) * LN], start=True, stop=True)
                elif stage == "l2":
                    wait_for(taken("l1", j))
                    for n in range(2):
                        last = mm(bank(k, n)[:, 0:LN], mlp_w[:, 2 + n, :], hid[:, j % 2, n, :], start=True, stop=True)
                elif stage == "t":
                    wait_for({})
                    if j % 2 == 0:
                        pe.wait_ge(d_ready, g * L_JOBS + -(-min(16 * (j // 2 + 1), KW) * KH // LN))
                    cols = [(j % 2, 16 * (j // 2) + 2 * i) for i in range(8)] if j < T_JOBS - 1 else [(0, KW - 2), (1, KW - 2)]
                    for i, (n, kw) in enumerate(cols):
                        last = nc.tensor.transpose(bank(k, i // 4)[:, (i % 4) * P:(i % 4 + 1) * P],
                                                   modes[:, n, kw * KH:(kw + 2) * KH], ident)
                else:
                    kw = I1_KW * j + I1_KW - 1
                    wait_for(taken("t", T_JOBS - 1 if kw == KW - 1 else 2 * (kw // 16) + 1))
                    v = V[:, I1_KW * j:I1_KW * (j + 1), :]
                    mm(bank(k, 0)[:, 0:I1_KW * P], g_hr, v, start=True, stop=True)
                    last = mm(bank(k, 1)[:, 0:I1_KW * P], g_hi, v, start=True, stop=True)
                last.then_inc(job_done, 1)

            constants_in(pe)
            with pe.Fori(0, B) as b:
                forward(pe, b, forward_job)
                for name in ("e_act", "e_dve"):
                    pe.wait_ge(evac[name], b * (CB * I1_JOBS) + (CREDIT[name] + CB * I1_JOBS))

                def inverse_w(m, n, first, blocks=range(CB)):
                    if blocks.stop == CB:
                        pe.wait_ge(et_in[n % 2], m * 8 + (16 if n % 2 == 0 else 8))
                    else:
                        pe.wait_ge(et_first_in, b * 16 + 16)
                    for k in blocks:
                        if not first:
                            pe.wait_ge(u_ready, m * CB - (CB - 1 - k))
                        for h in range(TH):
                            last = mm(ps[:, k, h * W:(h + 1) * W], et[:, n % 2, h, k * P:(k + 1) * P], g_w, start=True, stop=True)
                        last.then_inc(i2_done, 1)

                def mix(n, o, k):
                    w_hi, w_lo = fuse_hi[:, k, o * P:(o + 1) * P], fuse_lo[:, k, o * P:(o + 1) * P]
                    mm(ps[:, CB + o, :], w_hi, u_hi[:, n % 2, k, :], start=(k == 0), stop=False)
                    mm(ps[:, CB + o, :], w_hi, u_lo[:, n % 2, k, :], start=False, stop=False)
                    return mm(ps[:, CB + o, :], w_lo, u_hi[:, n % 2, k, :], start=False, stop=(k == CB - 1))

                def parts_ready(m, k):
                    pe.wait_ge(uhi_ready, m * CB + (k + 1))
                    pe.wait_ge(ulo_ready, m * CB + (k + 1))

                def mix_tiles(q, first, last_body):
                    for n in range(UN):
                        m = (b * TILES) + (q * UN + n)
                        if not (last_body and n == UN - 1):
                            inverse_w(m + 1, n + 1, False)
                        for o in range(CB):
                            if first and n == 0:
                                if o == 0:
                                    parts_ready(m, CB - 1)
                                mix(n, o, CB - 1).then_inc(mix_done, 1)
                                continue
                            pe.wait_ge(out_ready, m * CB - (CB - 1 - o))
                            for k in range(CB):
                                if o == 0:
                                    parts_ready(m, k)
                                last = mix(n, o, k)
                            last.then_inc(mix_done, 1)

                inverse_w(b * TILES, 0, True, range(CB - 1))
                pe.wait_ge(evac["e_act"], CREDIT["e_act"])
                pe.wait_ge(evac["e_dve"], CREDIT["e_dve"])
                pe.wait_ge(fuse_hi_ready, 1)
                pe.wait_ge(fuse_lo_ready, 1)
                for k in range(CB - 1):
                    parts_ready(b * TILES, k)
                    for o in range(CB):
                        mix(0, o, k)
                inverse_w(b * TILES, 0, True, range(CB - 1, CB))
                tile_bodies(pe, mix_tiles)
                pe.wait_ge(out_ready, (b + 1) * (TILES * CB))

        @block.scalar
        def _(act):
            copy = nc.scalar.activation

            def forward_job(jobs, base, b, cb, k):
                stage, j = jobs[k]
                g = b * CB + cb
                if stage == "none":
                    return
                act.wait_ge(job_done, base + jobs_up_to(jobs, k))
                if stage == "x":
                    if jobs is X_LIST and XH * (j + 1) * P > OT and XH * j * P <= OT:
                        output_stored(act, b)
                    copy(xT[:, XH * j:XH * j + 4, :], bank(k, 0), ACT.Copy).then_inc(evac["x_act"], 1)
                elif stage == "s1":
                    copy(Bw[:, 8 * j:8 * j + 4, :], s1_out(k, 0), ACT.Copy).then_inc(evac["b_act"], 1)
                elif stage == "s2":
                    z = slot(k, 0).rearrange("p (m r h) -> p r m h", r=2, h=KH)
                    n = min(8, KW - 8 * j)
                    copy(modes_k[0:64, 0, 8 * j:8 * j + n, :], z[:, 0, 0:n, :], ACT.Copy)
                    copy(modes_k[64:128, 0, 8 * j:8 * j + n, :], z[:, 1, 0:n, :], ACT.Copy).then_inc(evac["z_act"], 1)
                elif stage == "l1":
                    copy(hid[:, j % 2, 0, :], bank(k, 0)[:, 0:LN], ACT.Gelu, bias=mlp_b[:, 0:1])
                    copy(hid[:, j % 2, 1, :], bank(k, 1)[:, 0:LN], ACT.Gelu, bias=mlp_b[:, 1:2]).then_inc(evac["h_act"], 1)
                elif stage == "l2":
                    if j >= 2:
                        act.wait_ge(clip_ready, g * L_JOBS + (j - 1))
                        act.wait_ge(ymz_ready, g * L_JOBS + (j - 1))
                    copy(yt[:, j % 2, 0, :], bank(k, 0)[:, 0:LN], ACT.Identity, bias=mlp_b[:, 2:3])
                    copy(yt[:, j % 2, 1, :], bank(k, 1)[:, 0:LN], ACT.Identity, bias=mlp_b[:, 3:4]).then_inc(evac["y_act"], 1)
                elif stage == "t":
                    if j < T_JOBS - 1:
                        m, n = 16 * (j // 2), BS * (j % 2)
                        d = slot(k, 0).rearrange("p (i r c) -> p i r c", r=2, c=BS)
                        copy(V[0:64, m:m + 16:2, n:n + BS], d[:, :, 0, :], ACT.Copy)
                        copy(V[64:128, m:m + 16:2, n:n + BS], d[:, :, 1, :], ACT.Copy).then_inc(evac["v_act"], 1)
                else:
                    for n, (lo, _) in enumerate(EG):
                        if j == lo:
                            act.wait_ge(spilled[n], g * 32 + 16)
                    copy(E[:, 0, I1_KW * j:I1_KW * (j + 1), :], bank(k, 0)[:, 0:I1_KW * P], ACT.Copy).then_inc(evac["e_act"], 1)

            act.wait_ge(fuse_in, 16)
            copy(fuse_hi[:, 0:1, :], fuse_raw[:, 0:1, :], ACT.Copy).then_inc(evac["e_act"], CREDIT["e_act"])
            copy(fuse_hi[:, 1:CB, :], fuse_raw[:, 1:CB, :], ACT.Copy).then_inc(fuse_hi_ready, 1)
            act.wait_ge(evac["e_dve"], CREDIT["e_dve"])
            act.wait_ge(fuse_lo_ready, 1)
            with act.Fori(0, B) as b:
                forward(act, b, forward_job)

                def upper_u(m, n, reused):
                    for k in range(CB):
                        act.wait_ge(u_ready, m * CB + (k + 1))
                        if reused:
                            act.wait_ge(mix_done, m * CB - CB)
                        copy(u_hi[:, n % 2, k, :], u[:, (n % 2) * CB + k, :], ACT.Copy).then_inc(uhi_ready, 1)

                upper_u(b * TILES, 0, False)

                def tiles(q, first, last_body):
                    for n in range(UN):
                        m = (b * TILES) + (q * UN + n)
                        if not (last_body and n == UN - 1):
                            upper_u(m + 1, n + 1, not (first and n == 0))

                tile_bodies(act, tiles)
                act.wait_ge(out_ready, (b + 1) * (TILES * CB))

        @block.vector
        def _(dve):
            copy = nc.vector.tensor_copy

            def forward_job(jobs, base, b, cb, k):
                stage, j = jobs[k]
                g = b * CB + cb
                if stage in ("none", "l1"):
                    return
                if stage == "l2":
                    dve.wait_ge(evac["y_act"], g * L_JOBS + (j + 1))
                    if j:
                        dve.wait_ge(d_ready, g * L_JOBS + j)
                    nc.vector.tensor_scalar(clip[:, :, :], yt[:, j % 2, :, :], -LAM, LAM, ALU.max, ALU.min).then_inc(clip_ready, 1)
                    dve.wait_ge(clip_ready, g * L_JOBS + (j + 1))
                    dve.wait_ge(ymz_ready, g * L_JOBS + (j + 1))
                    nc.vector.tensor_tensor(modes[:, :, j * LN:(j + 1) * LN], ymz[:, j % 2, :, :], clip[:, :, :],
                                            ALU.subtract).then_inc(d_ready, 1)
                    return
                dve.wait_ge(job_done, base + jobs_up_to(jobs, k))
                if stage == "x":
                    if jobs is X_LIST and XH * (j + 1) * P > OT and XH * j * P <= OT:
                        output_stored(dve, b)
                    copy(xT[:, XH * j + 4:XH * j + 8, :], bank(k, 1)).then_inc(evac["x_dve"], 1)
                elif stage == "s1":
                    copy(Bw[:, 8 * j + 4:8 * j + 8, :], s1_out(k, 1)).then_inc(evac["b_dve"], 1)
                elif stage == "s2":
                    z = slot(k, 64).rearrange("p (m r h) -> p r m h", r=2, h=KH)
                    n = min(8, KW - 8 * j)
                    copy(modes_k[0:64, 1, 8 * j:8 * j + n, :], z[:, 0, 0:n, :])
                    copy(modes_k[64:128, 1, 8 * j:8 * j + n, :], z[:, 1, 0:n, :]).then_inc(evac["z_dve"], 1)
                elif stage == "t":
                    d = slot(k, 64).rearrange("p (i r c) -> p i r c", r=2, c=BS)
                    if j < T_JOBS - 1:
                        m, n = 16 * (j // 2), BS * (j % 2)
                        copy(V[0:64, m + 1:m + 16:2, n:n + BS], d[:, :, 0, :])
                        copy(V[64:128, m + 1:m + 16:2, n:n + BS], d[:, :, 1, :]).then_inc(evac["v_dve"], 1)
                    else:
                        v = V[:, KW - 1, :].rearrange("p (i c) -> p i c", c=BS)
                        copy(v[0:64], d[:, 0:2, 0, :])
                        copy(v[64:128], d[:, 0:2, 1, :]).then_inc(evac["v_dve"], 1)
                else:
                    for n, (lo, _) in enumerate(EG):
                        if j == lo:
                            dve.wait_ge(spilled[n], g * 32 + 16)
                    copy(E[:, 1, I1_KW * j:I1_KW * (j + 1), :], bank(k, 1)[:, 0:I1_KW * P]).then_inc(evac["e_dve"], 1)

            dve.wait_ge(fuse_hi_ready, 1)
            dve.wait_ge(evac["e_act"], CREDIT["e_act"])
            for part, signal, n in ((slice(0, 1), evac["e_dve"], CREDIT["e_dve"]), (slice(1, CB), fuse_lo_ready, 1)):
                nc.vector.tensor_tensor(fuse_lo[:, part, :], fuse_raw[:, part, :], fuse_hi[:, part, :].bitcast(fp32),
                                        ALU.subtract).then_inc(signal, n)
            dve.wait_ge(evac["e_dve"], CREDIT["e_dve"])
            dve.wait_ge(fuse_lo_ready, 1)
            with dve.Fori(0, B) as b:
                forward(dve, b, forward_job)

                def form_u(m, q16, n, reused, blocks=range(CB)):
                    dve.wait_ge(xt_in[n % UN], b * (TILES // UN * 16) + q16)
                    for k in blocks:
                        dve.wait_ge(i2_done, m * CB + (k + 1))
                        if reused:
                            dve.wait_ge(uhi_ready, m * CB - (2 * CB - 1 - k))
                            dve.wait_ge(ulo_ready, m * CB - (2 * CB - 1 - k))
                        nc.vector.tensor_tensor(u[:, (n % 2) * CB + k, :], ps[:, k, :], xt[:, n % UN, k, :], ALU.add).then_inc(u_ready, 1)
                    for k in blocks:
                        dve.wait_ge(uhi_ready, m * CB + (k + 1))
                        if reused:
                            dve.wait_ge(mix_done, m * CB - CB)
                        nc.vector.tensor_tensor(u_lo[:, n % 2, k, :], u[:, (n % 2) * CB + k, :], u_hi[:, n % 2, k, :].bitcast(fp32),
                                                ALU.subtract).then_inc(ulo_ready, 1)

                form_u(b * TILES, 16, 0, False, range(CB - 1))
                form_u(b * TILES, 16, 0, False, range(CB - 1, CB))

                def tiles(q, first, last_body):
                    for n in range(UN):
                        m = (b * TILES) + (q * UN + n)
                        if not (last_body and n == UN - 1):
                            form_u(m + 1, q * 16 + (16 if n < UN - 1 else 32), n + 1, not (first and n == 0))
                        if not first or n >= 2:
                            dve.wait_ge(stored[n % 2], m * 8 + (16 if n % 2 == 0 else 8))
                        for o in range(CB):
                            dve.wait_ge(mix_done, m * CB + (o + 1))
                            nc.vector.tensor_tensor(ot[:, n % 2, o, :], ps[:, CB + o, :], xt[:, n, o, :], ALU.add).then_inc(out_ready, 1)

                tile_bodies(dve, tiles)
                dve.wait_ge(out_ready, (b + 1) * (TILES * CB))

        @block.gpsimd
        def _(pool):
            parts = len(spilled + stored)
            for n, signal in enumerate(spilled + stored):
                part = slice(n * NCONST // parts, (n + 1) * NCONST // parts)
                pool.dma_start(cst[:, part], const[:, part]).then_inc(signal, 16)
            nc.gpsimd.memset(zero[:, :, :], 0.0).then_inc(zeroed, 1)
            pool.wait_ge(zeroed, 1)

            with pool.Fori(0, B) as b:
                with pool.Fori(0, CB) as cb:
                    g = b * CB + cb
                    pool.dma_start(mlp_w[:, :, :], mlp[cb, :, :, :]).then_inc(w_in, 16)
                    pool.dma_start(mlp_b[:, :], bias[cb, :, :]).then_inc(w_in, 16)
                    pool.wait_ge(w_in, g * 32 + 32)
                    nc.gpsimd.tensor_tensor(mlp_w[64:128, :, 0:BS], zero[64:128, :, :], mlp_w[64:128, :, 0:BS],
                                            ALU.subtract).then_inc(wneg_ready, 1)
                    for j in range(L_JOBS):
                        pool.wait_ge(evac["y_act"], g * L_JOBS + (j + 1))
                        if j >= 2:
                            pool.wait_ge(d_ready, g * L_JOBS + (j - 1))
                        nc.gpsimd.tensor_tensor(ymz[:, j % 2, :, :], yt[:, j % 2, :, :], modes[:, :, j * LN:(j + 1) * LN],
                                                ALU.subtract).then_inc(ymz_ready, 1)
                    for n, (lo, hi) in enumerate(EG):
                        for name in ("e_act", "e_dve"):
                            pool.wait_ge(evac[name], g * I1_JOBS + (CREDIT[name] + hi))
                        for ri in range(2):
                            pool.dma_start(spill[b, :, ri * KW + I1_KW * lo:ri * KW + I1_KW * hi, bass.ds(cb * P, P)],
                                           E[:, ri, I1_KW * lo:I1_KW * hi, :]).then_inc(spilled[n], 16)

                def tiles(q, first, last_body):
                    for n in range(UN):
                        m = (b * TILES) + (q * UN + n)
                        pool.wait_ge(out_ready, m * CB + CB)
                        pool.dma_start(out_pix[b, :, :, bass.ds(q * (UN * TP) + n * TP, TP)], ot[:, n % 2, :, :]).then_inc(stored[n % 2], 16)

                tile_bodies(pool, tiles)
            for n in range(2):
                pool.wait_ge(stored[n], 16 + B * TILES // 2 * 16)


def transform_constants():
    import numpy as np
    t = 2 * np.pi * np.outer(np.arange(H), np.arange(KH)) / H
    f = 2 * np.pi * np.outer(np.arange(W), np.arange(KW)) / W
    ck = np.where(np.arange(KW) == 0, 1.0, 2.0)[None, :]
    g_w = np.zeros((P, W))
    g_w[0:R2] = np.concatenate([(ck * np.cos(f)).T, -(ck * np.sin(f)).T], 0) / H
    parts = [np.concatenate([np.cos(f), -np.sin(f)], 1) / W,
             np.concatenate([np.cos(t), -np.sin(t)], 1), np.concatenate([np.sin(t), np.cos(t)], 1),
             np.concatenate([np.cos(t).T, -np.sin(t).T], 0), np.concatenate([np.sin(t).T, np.cos(t).T], 0),
             g_w, np.eye(P)]
    return np.concatenate(parts, 1).astype(np.float32)


def kernel(x, L0_conv_w1_real, L0_conv_w1_imag, L0_conv_b1_real, L0_conv_b1_imag,
           L0_conv_w2_real, L0_conv_w2_imag, L0_conv_b2_real, L0_conv_b2_imag, L0_conv_fuse_w):
    import numpy as np
    import concourse.bacc as bacc
    from concourse.bass_utils import run_bass_kernel_spmd

    def stacked(wr, wi):
        wr, wi = np.asarray(wr), np.asarray(wi)
        return np.concatenate([np.concatenate([wr, wi], 2), np.concatenate([wi, wr], 2)], 1)

    layers = [stacked(L0_conv_w1_real, L0_conv_w1_imag), stacked(L0_conv_w2_real, L0_conv_w2_imag)]
    mlp = np.stack([w.reshape(CB, 2, P, P) for w in layers], 1).transpose(0, 3, 1, 2, 4).reshape(CB, P, 4, P)
    biases = [np.concatenate([np.asarray(r), np.asarray(i)], 1) for r, i in
              ((L0_conv_b1_real, L0_conv_b1_imag), (L0_conv_b2_real, L0_conv_b2_imag))]
    bias = np.stack([v.reshape(CB, 2, P) for v in biases], 1).transpose(0, 3, 1, 2).reshape(CB, P, 4)
    arrays = {"x": x, "mlp": mlp, "bias": bias, "fuse_t": np.asarray(L0_conv_fuse_w).T, "const": transform_constants()}
    arrays = {n: np.ascontiguousarray(a) for n, a in arrays.items()}
    nc = bacc.Bacc("TRN2", target_bir_lowering=False, num_devices=1)
    aps = [nc.dram_tensor(n, a.shape, mybir.dt.float32, kind="ExternalInput").ap() for n, a in arrays.items()]
    out = nc.dram_tensor("out", (B, C, H, W), mybir.dt.float32, kind="ExternalOutput").ap()
    spill = nc.dram_tensor("spill", (B, H, R2, C), mybir.dt.float32, kind="Internal").ap()
    spectral_mix(nc, *aps, out, spill)
    r = run_bass_kernel_spmd(nc, [arrays], core_ids=[0])
    return r.results[0]["out"]
```
